# Optimizing a Trainium2 kernel written in Bass

```python
import numpy as np
import jax
import jax.numpy as jnp

def _softmax(x, axis=-1):
    return jax.nn.softmax(x, axis=axis)

def _gelu(x):
    return jax.nn.gelu(x, approximate=True)

def _silu(x):
    return jax.nn.silu(x)

def _sigmoid(x):
    return jax.nn.sigmoid(x)

def _layernorm(x, axis=-1, eps=1e-05):
    m = jnp.mean(x, axis=axis, keepdims=True)
    v = jnp.var(x, axis=axis, keepdims=True)
    return (x - m) / jnp.sqrt(v + eps)

def _scatter_add(tgt, idx, src, axis=0):
    return tgt.at[idx].add(src)

def _segment_sum(src, seg, n):
    return jax.ops.segment_sum(src, seg, n)
kernel_name = 'mk_seq_preln_d1_jaxref_r8_72e79f'

def setup_inputs(seed: int=0):
    np.random.seed(seed)
    _w = jnp.asarray

    def _L0_attn_setup():
        import math
        import jax, jax.numpy as jnp
        import numpy as np
        M_WIN = 64
        P = 8
        L_LEV = 4
        N_HEAD = 16

        def _pool(x, s):
            bh, n, d = x.shape
            return x.reshape(bh, n // s, s, d).mean(axis=2)

        def _shift_prev(xb):
            return jnp.pad(xb, ((0, 0), (1, 0), (0, 0), (0, 0)))[:, :-1]

        def _mla(q, k, v, m, p, L, scale_attn=True):
            bh, n, d = q.shape
            q = q / math.sqrt(d)
            Kls, Vls = ([k], [v])
            for l in range(L):
                s = m * 2 ** l // p
                Kls.append(_pool(k, s))
                Vls.append(_pool(v, s))
            nb = n // m
            Qc = q.reshape(bh, nb, m, d)
            Kc = k.reshape(bh, nb, m, d)
            Kwin = jnp.concatenate([_shift_prev(Kc), Kc], axis=2)
            S = jnp.einsum('bcqd,bckd->bcqk', Qc, Kwin)
            qg = jnp.broadcast_to(jnp.arange(m)[:, None], (m, m))
            kg = jnp.arange(m)[:, None] + 1 + jnp.arange(m)[None, :]
            As = [S[:, :, qg, kg].reshape(bh, n, m)]
            for l in range(1, L + 1):
                w = m * 2 ** (l - 1)
                nbl = n // w
                Kprev = _shift_prev(Kls[l].reshape(bh, nbl, p, d))
                Al = jnp.einsum('bcwd,bcpd->bcwp', q.reshape(bh, nbl, w, d), Kprev)
                As.append(Al.reshape(bh, n, p))
            maxes = jnp.stack([A.max(axis=-1) for A in As], axis=-1)
            mn = maxes.min(axis=-1, keepdims=True)
            exps = [jnp.exp(A - mn) for A in As]
            scales = [1] + [m * 2 ** (l - 1) // p for l in range(1, L + 1)]
            esum = exps[0].sum(axis=-1)
            for l in range(1, L + 1):
                s_l = exps[l].sum(axis=-1)
                esum = esum + (s_l * scales[l] if scale_attn else s_l)
            esum = esum[..., None]
            Cs = [(scales[l] if l > 0 and scale_attn else 1) * exps[l] / esum for l in range(L + 1)]
            C0 = Cs[0].reshape(bh, nb, m, m)
            Cfull = jnp.zeros((bh, nb, m, 2 * m), C0.dtype).at[:, :, qg, kg].set(C0)
            Vc = v.reshape(bh, nb, m, d)
            Vwin = jnp.concatenate([_shift_prev(Vc), Vc], axis=2)
            out = jnp.einsum('bcqk,bckd->bcqd', Cfull, Vwin).reshape(bh, n, d)
            for l in range(1, L + 1):
                w = m * 2 ** (l - 1)
                nbl = n // w
                Vprev = _shift_prev(Vls[l].reshape(bh, nbl, p, d))
                out = out + jnp.einsum('bcwp,bcpd->bcwd', Cs[l].reshape(bh, nbl, w, p), Vprev).reshape(bh, n, d)
            return out
        key = jax.random.key(seed)
        ks = jax.random.split(key, 4)
        B, T, C = (8, 256, 128)
        x = jax.random.normal(ks[0], (B, T, C), jnp.float32)
        W_attn = jax.random.normal(ks[1], (C, 3 * C), jnp.float32) * 0.02
        b_attn = jnp.zeros((3 * C,), jnp.float32)
        W_proj = jax.random.normal(ks[2], (C, C), jnp.float32) * 0.02
        b_proj = jnp.zeros((C,), jnp.float32)
        return {'x': x, 'W_attn': W_attn, 'b_attn': b_attn, 'W_proj': W_proj, 'b_proj': b_proj}
    _L0_attn_in = _L0_attn_setup()

    def _L0_ffn_setup():
        import jax, jax.numpy as jnp
        import numpy as np
        TOP_K = 2
        EPS = 1e-09
        key = jax.random.key(seed)
        ks = jax.random.split(key, 6)
        B, T, D, H, E = (4, 256, 128, 256, 8)
        x = jax.random.normal(ks[0], (B, T, D), dtype=jnp.float32)
        Wg = jax.random.normal(ks[1], (E, D), dtype=jnp.float32) * 0.02
        W1 = jax.random.normal(ks[2], (E, 2 * H, D), dtype=jnp.float32) * 0.02
        b1 = jax.random.normal(ks[3], (E, 2 * H), dtype=jnp.float32) * 0.02
        Wo = jax.random.normal(ks[4], (D, H), dtype=jnp.float32) * 0.02
        bo = jax.random.normal(ks[5], (D,), dtype=jnp.float32) * 0.02
        return {'x': x, 'Wg': Wg, 'W1': W1, 'b1': b1, 'Wo': Wo, 'bo': bo}
    _L0_ffn_in = _L0_ffn_setup()
    _d = {'L0_attn_x': _L0_attn_in['x'], 'L0_attn_W_attn': _L0_attn_in['W_attn'], 'L0_attn_b_attn': _L0_attn_in['b_attn'], 'L0_attn_W_proj': _L0_attn_in['W_proj'], 'L0_attn_b_proj': _L0_attn_in['b_proj'], 'L0_ffn_Wg': _L0_ffn_in['Wg'], 'L0_ffn_W1': _L0_ffn_in['W1'], 'L0_ffn_b1': _L0_ffn_in['b1'], 'L0_ffn_Wo': _L0_ffn_in['Wo'], 'L0_ffn_bo': _L0_ffn_in['bo']}
    _x0 = _d['L0_attn_x']
    _d['L0_attn_x'] = jax.random.normal(jax.random.fold_in(jax.random.key(seed), 1), (2, 1024, 128), dtype=_x0.dtype)
    del _x0
    return _d

def reference(L0_attn_x, L0_attn_W_attn, L0_attn_b_attn, L0_attn_W_proj, L0_attn_b_proj, L0_ffn_Wg, L0_ffn_W1, L0_ffn_b1, L0_ffn_Wo, L0_ffn_bo):

    def _L0_attn_ref(x, W_attn, b_attn, W_proj, b_proj):
        import math
        import jax, jax.numpy as jnp
        import numpy as np
        M_WIN = 64
        P = 8
        L_LEV = 4
        N_HEAD = 16

        def _pool(x, s):
            bh, n, d = x.shape
            return x.reshape(bh, n // s, s, d).mean(axis=2)

        def _shift_prev(xb):
            return jnp.pad(xb, ((0, 0), (1, 0), (0, 0), (0, 0)))[:, :-1]

        def _mla(q, k, v, m, p, L, scale_attn=True):
            bh, n, d = q.shape
            q = q / math.sqrt(d)
            Kls, Vls = ([k], [v])
            for l in range(L):
                s = m * 2 ** l // p
                Kls.append(_pool(k, s))
                Vls.append(_pool(v, s))
            nb = n // m
            Qc = q.reshape(bh, nb, m, d)
            Kc = k.reshape(bh, nb, m, d)
            Kwin = jnp.concatenate([_shift_prev(Kc), Kc], axis=2)
            S = jnp.einsum('bcqd,bckd->bcqk', Qc, Kwin)
            qg = jnp.broadcast_to(jnp.arange(m)[:, None], (m, m))
            kg = jnp.arange(m)[:, None] + 1 + jnp.arange(m)[None, :]
            As = [S[:, :, qg, kg].reshape(bh, n, m)]
            for l in range(1, L + 1):
                w = m * 2 ** (l - 1)
                nbl = n // w
                Kprev = _shift_prev(Kls[l].reshape(bh, nbl, p, d))
                Al = jnp.einsum('bcwd,bcpd->bcwp', q.reshape(bh, nbl, w, d), Kprev)
                As.append(Al.reshape(bh, n, p))
            maxes = jnp.stack([A.max(axis=-1) for A in As], axis=-1)
            mn = maxes.min(axis=-1, keepdims=True)
            exps = [jnp.exp(A - mn) for A in As]
            scales = [1] + [m * 2 ** (l - 1) // p for l in range(1, L + 1)]
            esum = exps[0].sum(axis=-1)
            for l in range(1, L + 1):
                s_l = exps[l].sum(axis=-1)
                esum = esum + (s_l * scales[l] if scale_attn else s_l)
            esum = esum[..., None]
            Cs = [(scales[l] if l > 0 and scale_attn else 1) * exps[l] / esum for l in range(L + 1)]
            C0 = Cs[0].reshape(bh, nb, m, m)
            Cfull = jnp.zeros((bh, nb, m, 2 * m), C0.dtype).at[:, :, qg, kg].set(C0)
            Vc = v.reshape(bh, nb, m, d)
            Vwin = jnp.concatenate([_shift_prev(Vc), Vc], axis=2)
            out = jnp.einsum('bcqk,bckd->bcqd', Cfull, Vwin).reshape(bh, n, d)
            for l in range(1, L + 1):
                w = m * 2 ** (l - 1)
                nbl = n // w
                Vprev = _shift_prev(Vls[l].reshape(bh, nbl, p, d))
                out = out + jnp.einsum('bcwp,bcpd->bcwd', Cs[l].reshape(bh, nbl, w, p), Vprev).reshape(bh, n, d)
            return out
        B, T, C = x.shape
        H = N_HEAD
        dh = C // H
        qkv = x @ W_attn + b_attn
        q, k, v = jnp.split(qkv, 3, axis=2)

        def heads(t):
            return t.reshape(B, T, H, dh).transpose(0, 2, 1, 3).reshape(B * H, T, dh)
        o = _mla(heads(q), heads(k), heads(v), M_WIN, P, L_LEV, scale_attn=True)
        o = o.reshape(B, H, T, dh).transpose(0, 2, 1, 3).reshape(B, T, C)
        return o @ W_proj + b_proj

    def _L0_ffn_ref(x, Wg, W1, b1, Wo, bo):
        import jax, jax.numpy as jnp
        import numpy as np
        TOP_K = 2
        EPS = 1e-09
        E = Wg.shape[0]
        gate_logits = jnp.einsum('btd,ed->bte', x, Wg)
        gate_scores = jax.nn.softmax(gate_logits, axis=-1)
        topk_val, topk_idx = jax.lax.top_k(gate_scores, TOP_K)
        topk_val = topk_val / (topk_val.sum(axis=-1, keepdims=True) + EPS)
        comb = (jax.nn.one_hot(topk_idx, E, dtype=x.dtype) * topk_val[..., None]).sum(axis=-2)
        out = jnp.zeros_like(x)
        for e in range(E):
            h = jnp.einsum('btd,hd->bth', x, W1[e]) + b1[e]
            a, b = jnp.split(h, 2, axis=-1)
            g = a * jax.nn.sigmoid(b)
            eo = jnp.einsum('bth,dh->btd', g, Wo) + bo
            out = out + eo * comb[..., e:e + 1]
        return out
    x = L0_attn_x
    x = x + _L0_attn_ref(_layernorm(x, axis=-1), L0_attn_W_attn, L0_attn_b_attn, L0_attn_W_proj, L0_attn_b_proj)
    x = x + _L0_ffn_ref(_layernorm(x, axis=-1), L0_ffn_Wg, L0_ffn_W1, L0_ffn_b1, L0_ffn_Wo, L0_ffn_bo)
    return x

_drawn_inputs = setup_inputs


def setup_inputs(seed=0):
    import zlib

    import numpy as np

    out = dict(_drawn_inputs(seed))
    spreads = {'L0_attn_b_attn': (0.0, 0.497), 'L0_attn_b_proj': (0.0, 0.1)}
    factors = {'L0_attn_W_attn': 8.0,
     'L0_attn_W_proj': 3.881,
     'L0_ffn_b1': 32.056,
     'L0_ffn_Wg': 2.683,
     'L0_ffn_W1': 2.9,
     'L0_ffn_bo': 3.233}
    for name, (base, spread) in spreads.items():
        noise = np.random.default_rng([zlib.crc32(name.encode()), seed]).standard_normal(out[name].shape)
        drawn = base * np.exp(spread * noise) if base else spread * noise
        out[name] = jnp.asarray(drawn.astype(out[name].dtype))
    for name, factor in factors.items():
        out[name] = (out[name] * factor).astype(out[name].dtype)
    return out
```

```python
import concourse.bass as bass
from concourse import mybir
from contextlib import ExitStack

F32 = mybir.dt.float32
F32R = mybir.dt.float32r
BF16 = mybir.dt.bfloat16
U32 = mybir.dt.uint32
ALU = mybir.AluOpType
ACT = mybir.ActivationFunctionType
AX = mybir.AxisListType

P = 128
B, T, C = 2, 1024, 128
H, DH = 16, 8
WIN, POOLED, LEVELS = 64, 8, 4
NB = T // WIN
GH = 4
NG = H // GH
UNITS = B * NG
LK = LEVELS * POOLED
TT = T // P
SLOTS = 3
SR = SLOTS * GH * DH
E, HID = 8, 256
TOPK = 2
LN_EPS, GATE_EPS = 1e-5, 1e-9
QSCALE = 1.0 / float(DH) ** 0.5
MASKED = -1.0e30
PAD = WIN

C_IDENT = 0
C_BAND = C_IDENT + P
C_PADMASK = C_BAND + WIN
C_POOLW = C_PADMASK + NB * LK
C_DEN = C_POOLW + 1
C_IOTA = C_DEN + GH * DH
C_NONPAD = C_IOTA + E
C_ONES = C_NONPAD + NB * LK
C_FIRST = C_ONES + P
C_SEL = C_FIRST + P
C_HEAD = C_SEL + 2
C_COLS = C_HEAD + GH


def shape_constants(np):
    c = np.zeros((P, C_COLS), np.float32)
    c[:, C_IDENT:C_IDENT + P] = np.eye(P)
    key, qry = np.arange(P)[:, None], np.arange(WIN)[None, :]
    c[:, C_BAND:C_BAND + WIN] = np.where((key > qry) & (key <= qry + WIN), 0.0, MASKED)
    blk, lev = np.arange(NB)[:, None, None], np.arange(LEVELS)[None, :, None]
    real = np.broadcast_to(blk >= 2 ** lev, (NB, LEVELS, POOLED)).reshape(-1)
    c[:, C_PADMASK:C_PADMASK + NB * LK] = real
    weight = POOLED * 2.0 ** ((np.arange(P) % LK) // POOLED)
    c[:, C_POOLW] = weight
    for j in range(GH):
        c[j * LK:(j + 1) * LK, C_DEN + j * DH:C_DEN + (j + 1) * DH] = weight[:LK, None]
    c[:, C_IOTA:C_IOTA + E] = np.arange(E)
    c[0:2, C_NONPAD:C_NONPAD + NB * LK] = real
    c[0:2, C_ONES:C_ONES + P] = 1.0
    c[0:2, C_FIRST + WIN:C_FIRST + P] = 1.0
    c[0, C_SEL], c[1, C_SEL + 1] = 1.0, 1.0
    for r in range(2 * GH):
        c[SR + r, C_HEAD + r % GH] = 1.0
    return c


GENERAL = {"bias", "xT", "qk", "kp", "v", "pv", "guard", "shiftT", "proj", "w1", "w2", "x2T", "gatelog", "hidT", "y"}
ACT_LAST = {"v", "hidT"}
ACT_FIRST = {"xT", "qk", "w1", "x2T"}
SPU = 2 + NB // 2


def schedule():
    s = [("bias",), ("ln1", 0), ("xT", 0, 0), ("xT", 0, 1), ("pool", 0)]
    s += [("qk", 0, t, n) for t in range(2) for n in range(2)] + [("kp", 0), ("ln1", 1)]
    s += [("v", 0, n) for n in range(4)] + [("pv", 0, n) for n in range(4)]
    s += [("guard", 0, m) for m in range(4)] + [("shift", 0), ("shiftT", 0)]
    local = []
    for u in range(UNITS):
        last_b0 = u == NG - 1
        prep1 = [("xT", 1, 0), ("xT", 1, 1), ("pool", 1)] + [("qk", 1, t, n) for t in range(2) for n in range(2)] + [("kp", 1)]
        for i in range(SPU):
            s.append(("score", u, i))
            if i >= 2:
                local.append((u, i - 2))
            if len(local) > 2:
                s.append(("out",) + local.pop(0))
                if s[-1][2] % 4 == 3:
                    s.append(("norm", s[-1][1], s[-1][2] // 4))
            if last_b0:
                if i < 5:
                    s += {0: prep1[0:2], 1: prep1[2:4], 2: prep1[4:5], 3: prep1[5:7], 4: prep1[7:8]}[i]
            elif u + 1 < UNITS:
                if 1 <= i <= 4:
                    s.append(("guard", u + 1, i - 1))
                if i == 4:
                    s.append(("shift", u + 1))
                if i == 6:
                    s.append(("shiftT", u + 1))
            if u == NG and i == 5:
                s += [("ln2", 0, 0), ("ln2", 0, 1)]
            if u == NG and i in (7, 8):
                s.append(("x2T", 0, i - 7))
            if u == UNITS - 2 and i == 8:
                s.append(("w2",))
            if u == UNITS - 1:
                s += {1: [("gatelog", 0)], 2: [("gate", 0)]}.get(i, [])
                if i >= 2:
                    s.append(("w1", i - 2))
        if last_b0 or u == UNITS - 1:
            while local:
                s.append(("out",) + local.pop(0))
                if s[-1][2] % 4 == 3:
                    s.append(("norm", s[-1][1], s[-1][2] // 4))
        if last_b0:
            s += [("guard", u + 1, m) for m in range(4)] + [("shift", u + 1)]
            s += [("v", 1, n) for n in range(4)] + [("shiftT", u + 1)] + [("pv", 1, n) for n in range(4)]
            s += [("proj", 0, 0), ("proj", 0, 1)]
    s += [("proj", 1, 0), ("proj", 1, 1)]
    extra = {(0, 0): [("ln2", 1, 0)], (0, 2): [("ln2", 1, 1)], (1, 4): [("x2T", 1, 0)], (1, 6): [("x2T", 1, 1)],
             (2, 1): [("gatelog", 1)], (2, 3): [("gate", 1)]}
    for t in range(B * TT):
        for e in range(E):
            s.append(("hidden", t, e))
            s += extra.get((t, e), [])
            if t and e == 2:
                s.append(("hidT", t - 1))
            if t and e == 4:
                s.append(("y", t - 1))
    return s + [("hidT", B * TT - 1), ("y", B * TT - 1)]


SCHEDULE = schedule()
GEN = [s for s in SCHEDULE if s[0] in GENERAL]
GEN_AT = {s: n for n, s in enumerate(GEN)}
GEN_BANKS = 3
SCORE_BANKS = 3
HID_BANKS = 5
P_RING = 4
SIG_RING = 3
TMP_RING = 4


def build(nc, x_d, wattn_d, battn_d, wproj_d, bproj_d, wg_d, w1_d, b1_d, wo_d, bo_d, const_d, out_d):
    ctx = ExitStack()
    with ctx:
        def sb(name, shape, dt=F32):
            return ctx.enter_context(nc.sbuf_tensor(name, shape, dt))

        def sem(name):
            return ctx.enter_context(nc.semaphore(name))

        const = sb("const", [P, C_COLS])
        ident = const[:, C_IDENT:C_IDENT + P]
        ident_bf = sb("ident_bf", [P, P], BF16)
        band_bf = sb("band_bf", [P, WIN], BF16)
        rows2 = sb("rows2", [2, NB * LK + 2 * P], F32R)
        bv2 = sb("bv2", [2, C], F32R)
        bv_raw = sb("bv_raw", [2, C])
        bv_hi = sb("bv_hi", [2, C], F32R)
        bv_lo = sb("bv_lo", [2, C])
        xres = sb("xres", [P, B * TT, C])
        xnorm = sb("xnorm", [P, B * TT, C])
        attT = sb("attT", [P, T])
        rden = sb("rden", [P, 4 * P])
        wattn = attT[:, 0:3 * C]
        wqkv = attT[:, 3 * C:6 * C]
        wqkv_hi = sb("wqkv_hi", [P, 3 * C], F32R)
        wqkv_lo = sb("wqkv_lo", [P, 3 * C], F32R)
        bias_row = rden[0:1, 0:3 * C]
        b1_rows = rden[0:4 * E, 3 * C:4 * C]
        bias_perm = attT[0:1, 6 * C:8 * C]
        bias_col = sb("bias_col", [P, 2])
        wproj = sb("wproj", [P, C])
        bproj_b = sb("bproj_b", [P, C])
        bo_b = sb("bo_b", [P, C])
        xT_hi = sb("xT_hi", [P, PAD + T], F32R)
        xT_lo = sb("xT_lo", [P, PAD + T], F32R)
        pool_sum = [sb(f"pool_sum{l}", [P, T // (POOLED << l)]) for l in range(LEVELS)]
        xpool = sb("xpool", [P, NB, LEVELS, POOLED])
        xpool_hi = sb("xpool_hi", [P, NB, LK], F32R)
        xpool_lo = sb("xpool_lo", [P, NB, LK], F32R)
        arena = sb("arena", [P, 4, T], F32R)
        q_hi, q_lo, k_hi, k_lo = (arena[:, n, :] for n in range(4))
        kpool = sb("kpool", [P, NB * LK])
        kpool_hi = sb("kpool_hi", [P, NB * LK], F32R)
        kpool_lo = sb("kpool_lo", [P, NB * LK], F32R)
        vwin = sb("vwin", [P, NB, C])
        vpool = sb("vpool", [P, NB, NG, WIN])
        qst = [sb(f"qst{i}", [P, T], F32R) for i in range(2)]
        qmk = [sb(f"qmk{i}", [P, GH, T], F32R) for i in range(2)]
        kst = [sb(f"kst{i}", [P, PAD + T], F32R) for i in range(2)]
        pks = sb("pks", [SR, NB * LK], F32R)
        pkm = [sb(f"pkm{i}", [P, NB, GH, LK], F32R) for i in range(2)]
        vaug = [sb(f"vaug{i}", [P, NB // 2, GH, WIN]) for i in range(2)]
        work = sb("work", [P, P_RING * 512 + 2 * NB * WIN])
        prob = [work[:, i * 512:(i + 1) * 512].rearrange("p (c j q) -> p c j q", c=2, j=GH) for i in range(P_RING)]
        probp = [work[:, P_RING * 512 + i * T:P_RING * 512 + (i + 1) * T].rearrange("p (c q) -> p c q", q=WIN) for i in range(2)]
        lmax = sb("lmax", [P, TT, GH, LEVELS])
        nshift = sb("nshift", [P, GH, TT])
        nshift_hi = sb("nshift_hi", [GH * TT, P], F32R)
        nshift_lo = sb("nshift_lo", [GH * TT, P], F32R)
        stats = sb("stats", [P, TT, 6])
        mv = sb("mv", [P, TT, 2])
        veps = sb("veps", [P, TT])
        rstd = sb("rstd", [P, TT])
        nhalf = sb("nhalf", [P, TT])
        w1_stage = [xpool[:, :, :, :].rearrange("p (t a) l k -> p t (a l k)", t=4), kpool[:, :].rearrange("p (t c) -> p t c", t=4)]
        b1_col = sb("b1_col", [P, 4 * E])
        w1T_hi = qmk[0][:, :, :].rearrange("p a (b n) -> p (a b) n", b=2)
        w1T_lo = arena[:, :, :].rearrange("p a (b n) -> p (a b) n", b=2)
        wo_raw = sb("wo_raw", [P, HID])
        woT = sb("woT", [P, 2, C])
        wg_raw = sb("wg_raw", [E, C])
        wgT = sb("wgT", [P, E])
        wgT_hi = sb("wgT_hi", [P, E], F32R)
        wgT_lo = sb("wgT_lo", [P, E], F32R)
        x2T = [(xT_hi, xT_lo), (kst[0], kst[1])]
        glog = sb("glog", [P, TT, E])
        gtop = sb("gtop", [P, TT, 8])
        gidx = sb("gidx", [P, TT, 8], U32)
        gidx_f = sb("gidx_f", [P, TT, TOPK])
        gexp = sb("gexp", [P, TT, E])
        gsel = sb("gsel", [P, 2, TT, E])
        gsum = sb("gsum", [P, 4, TT])
        comb = sb("comb", [P, B * TT, E])
        csum = sb("csum", [P, B * TT])
        ring = [work[:, i * HID:(i + 1) * HID] for i in range(SIG_RING + TMP_RING + 4)]
        sig, gtmp = ring[0:SIG_RING], ring[SIG_RING:SIG_RING + TMP_RING]
        gacc = ring[SIG_RING + TMP_RING:SIG_RING + TMP_RING + 2]
        hidT = [r.rearrange("p (a q) -> p a q", a=2) for r in ring[SIG_RING + TMP_RING + 2:]]
        ybias = sb("ybias", [P, C])
        yout = [sb(f"yout{i}", [P, C]) for i in range(2)]

        bank = [ctx.enter_context(nc.psum_tensor(f"bank{i}", [P, 512], F32)) for i in range(8)]

        def gen_bank(step):
            return bank[5 + GEN_AT[step] % GEN_BANKS]

        x_in = [sem(f"x_in{b}") for b in range(B)]
        const_in, wattn_in, late_in = sem("const_in"), sem("wattn_in"), sem("late_in")
        w1_in = [sem(f"w1_in{i}") for i in range(2)]
        cst_ready = sem("cst_ready")
        zero_ready = sem("zero_ready")
        wqkv_ready = sem("wqkv_ready")
        gen_full = sem("gen_full")
        gen_hi = sem("gen_hi")
        gen_dve = sem("gen_dve")
        gen_act = sem("gen_act")
        veps_ready, rstd_ready, xn_ready, ln2_ready = sem("veps_ready"), sem("rstd_ready"), sem("xn_ready"), sem("ln2_ready")
        xb_ready = sem("xb_ready")
        pool_ready, shift_ready = sem("pool_ready"), sem("shift_ready")
        qst_in = [sem(f"qst_in{i}") for i in range(2)]
        kst_in = [sem(f"kst_in{i}") for i in range(2)]
        qmk_in = [sem(f"qmk_in{i}") for i in range(2)]
        pkm_in = [sem(f"pkm_in{i}") for i in range(2)]
        shift_in = [sem(f"shift_in{i}") for i in range(2)]
        pks_in = sem("pks_in")
        score_full, exp_done, out_done, norm_done, vaug_ready = (sem(n) for n in ("score_full", "exp_done", "out_done", "norm_done", "vaug_ready"))
        w1_fixed = sem("w1_fixed")
        gl_ready, gsub_ready, gexp_ready, comb_ready = (sem(n) for n in ("gl_ready", "gsub_ready", "gexp_ready", "comb_ready"))
        hid_full, sig_done, hid_done, acc_done = (sem(n) for n in ("hid_full", "sig_done", "hid_done", "acc_done"))
        out_sent = [sem(f"out_sent{i}") for i in range(2)]
        dve_step, pool_step = sem("dve_step"), sem("pool_step")

        def wait_gen_done(eng, step):
            kind = step[0] in ACT_LAST
            n = sum((s[0] in ACT_LAST) == kind for s in GEN[:GEN_AT[step] + 1])
            eng.wait_ge(gen_act if kind else gen_dve, n)

        def wait_gen_full(eng, step):
            eng.wait_ge(gen_full, GEN_AT[step] + 1)

        def wait_gen_hi(eng, step):
            eng.wait_ge(gen_hi, sum(s[0] in ACT_FIRST for s in GEN[:GEN_AT[step] + 1]))

        def wait_unit_loads(eng, u, *sems):
            for pair, n in sems:
                eng.wait_ge(pair[u % 2], 16 * n * (u // 2 + 1))

        QST, KST, QMK, PKM, SHIFT = (qst_in, 3), (kst_in, 3), (qmk_in, 4), (pkm_in, 4), (shift_in, 4)

        block = ctx.enter_context(nc.Block())

        @block.sync
        def _(sp):
            xv = x_d.rearrange("b (t p) c -> b p t c", p=P)
            sp.dma_start(xres[:, 0:TT // 2, :], xv[0, :, 0:TT // 2, :]).then_inc(x_in[0], 16)
            sp.dma_start(xres[:, TT // 2:TT, :], xv[0, :, TT // 2:TT, :]).then_inc(x_in[0], 16)
            sp.dma_start(const[:, :], const_d).then_inc(const_in, 16)
            sp.dma_start(xres[:, TT:2 * TT, :], xv[1]).then_inc(x_in[1], 16)
            sp.dma_start(wproj[:, :], wproj_d).then_inc(late_in, 16)
            sp.dma_start(bproj_b[:, :], bproj_d.partition_broadcast(P)).then_inc(late_in, 16)
            sp.dma_start(bo_b[:, :], bo_d.partition_broadcast(P)).then_inc(late_in, 16)
            sp.dma_start(wo_raw[:, :], wo_d).then_inc(late_in, 16)
            sp.dma_start(wg_raw[:, :], wg_d).then_inc(late_in, 16)

            def move(dst, src):
                return sp.dma_start(dst.bitcast(F32), src.bitcast(F32))

            def load_stacks(u):
                b, g, s = u // NG, u % NG, u % 2
                rows = slice(g * GH * DH, (g + 1) * GH * DH)
                wait_gen_done(sp, ("qk", b, 1, 1))
                wait_gen_done(sp, ("kp", b))
                if u < 2:
                    sp.wait_ge(zero_ready, 1 + u)
                else:
                    sp.wait_ge(score_full, (u - 2) * SPU + 2)
                for n, src in enumerate((q_hi, q_hi, q_lo)):
                    move(qst[s][n * 32:(n + 1) * 32, :], src[rows, :]).then_inc(qst_in[s], 16)
                if u:
                    wait_unit_loads(sp, u - 1, PKM)
                for n, src in enumerate((kpool_hi, kpool_lo, kpool_hi)):
                    move(pks[n * 32:(n + 1) * 32, :], src[rows, :]).then_inc(pks_in, 16)
                sp.wait_ge(pks_in, 48 * (u + 1))
                for j in range(GH):
                    move(pkm[s][j:SR:GH, :, j, :], pks[j:SR:GH, :].rearrange("p (c k) -> p c k", k=LK)).then_inc(pkm_in[s], 16)

            def load_local(u):
                g, s = u % NG, u % 2
                rows = slice(g * GH * DH, (g + 1) * GH * DH)
                if u >= 2:
                    sp.wait_ge(score_full, (u - 1) * SPU)
                for n, src in enumerate((k_hi, k_lo, k_hi)):
                    move(kst[s][n * 32:(n + 1) * 32, PAD:], src[rows, :]).then_inc(kst_in[s], 16)
                wait_unit_loads(sp, u, QST)
                for j in range(GH):
                    move(qmk[s][j:SR:GH, j, :], qst[s][j:SR:GH, :]).then_inc(qmk_in[s], 16)

            def load_shift(u):
                s = u % 2
                wait_gen_done(sp, ("shiftT", u))
                for n, src in enumerate((nshift_hi, nshift_lo)):
                    move(qmk[s][SR + n:SR + n + 1, :, :].rearrange("p j (i q) -> p (j i) q", q=P), src[:, :])\
                      .then_inc(shift_in[s], 16)
                    move(qst[s][SR + n * GH:SR + (n + 1) * GH, :].rearrange("p (i q) -> p i q", q=P), src[:, :])\
                      .then_inc(shift_in[s], 16)

            load_stacks(0)
            for u in range(UNITS):
                load_local(u)
                if u + 1 < UNITS and u + 1 != NG:
                    load_stacks(u + 1)
                load_shift(u)
                if u + 1 == NG:
                    load_stacks(u + 1)
                if u == NG:
                    wait_gen_full(sp, ("pv", 1, 3))
                    for i in range(2):
                        sp.dma_start(w1_stage[i], w1_d[i].rearrange("(t p) c -> p t c", p=P)).then_inc(w1_in[i], 16)
            for n in range(2, E):
                wait_gen_done(sp, ("w1", n - 2))
                sp.dma_start(w1_stage[n % 2], w1_d[n].rearrange("(t p) c -> p t c", p=P)).then_inc(w1_in[n % 2], 16)
            for t in range(B * TT):
                wait_gen_done(sp, ("y", t))
                sp.dma_start(out_d[t // TT, (t % TT) * P:(t % TT + 1) * P, :], yout[t % 2][:, :]).then_inc(out_sent[t % 2], 16)
            for i in range(2):
                sp.wait_ge(out_sent[i], 16 * B * TT // 2)

        @block.gpsimd
        def _(gp):
            steps = [0]

            def then(ins):
                steps[0] += 1
                ins.then_inc(pool_step, 1)
                gp.wait_ge(pool_step, steps[0])

            then(gp.memset(nhalf[:, :], -0.5))

            def rstd_of(n, cols):
                gp.wait_ge(veps_ready, n)
                gp.tensor_tensor(rstd[:, cols], veps[:, cols], nhalf[:, cols], ALU.pow).then_inc(rstd_ready, 1)

            def add_bproj(b):
                gp.wait_ge(xn_ready, b + 1)
                gp.wait_ge(late_in, 80)
                gp.tensor_tensor(xres[:, b * TT:(b + 1) * TT, :], xres[:, b * TT:(b + 1) * TT, :],
                                 bproj_b[:, :].unsqueeze(1).broadcast_to([P, TT, C]), ALU.add).then_inc(xb_ready, 1)

            def values_of(hu):
                u, h = hu // 2, hu % 2
                b, g = u // NG, u % NG
                if hu == 0 or hu == UNITS:
                    for n in range(4):
                        wait_gen_done(gp, ("v", b, n))
                if hu >= 2:
                    gp.wait_ge(out_done, 4 * (hu - 1))
                half = NB // 2
                for j in range(GH):
                    c0 = (g * GH + j) * DH
                    ins = gp.tensor_copy(vaug[hu % 2][:, :, j, j * DH:(j + 1) * DH], vwin[:, h * half:(h + 1) * half, c0:c0 + DH])
                ins.then_inc(vaug_ready, 1)

            for i in range(2):
                gp.memset(kst[i][:, :].bitcast(F32), 0.0)
                gp.memset(pkm[i][:, :, :, :].bitcast(F32), 0.0)
                then(gp.memset(qmk[i][:, :, :].bitcast(F32), 0.0))
                if i == 0:
                    gp.wait_ge(const_in, 16)
                then(gp.memset(kst[i][SR:SR + 2, :].bitcast(F32), 1.0))
                for j in range(GH):
                    ins = gp.tensor_copy(pkm[i][SR:SR + 2 * GH, :, j, :],
                                         const[SR:SR + 2 * GH, C_HEAD + j:C_HEAD + j + 1].unsqueeze(2).broadcast_to([2 * GH, NB, LK]))
                ins.then_inc(zero_ready, 1)
                gp.wait_ge(zero_ready, i + 1)
                if i == 0:
                    rstd_of(1, slice(0, TT))
            rstd_of(2, slice(0, TT))
            for i in range(2):
                then(gp.memset(vaug[i][:, :, :, :], 0.0))
                for j in range(GH):
                    ins = gp.memset(vaug[i][:, :, j, 32 + j * DH:32 + (j + 1) * DH], 1.0)
                then(ins)
            add_bproj(0)
            add_bproj(1)
            values_of(0)
            values_of(1)
            n_ln2 = 0

            def fix_w1(n):
                st = w1_stage[n % 2]
                wait_gen_done(gp, ("bias",))
                gp.wait_ge(w1_in[n % 2], 16 * (n // 2 + 1))
                then(gp.tensor_tensor(st[:, :, 0:C - 1], st[:, :, 0:C - 1], st[:, :, C - 1:C].broadcast_to([P, 4, C - 1]), ALU.subtract))
                gp.tensor_copy(st[:, :, C - 1:C], b1_col[:, 4 * n:4 * n + 4].unsqueeze(2)).then_inc(w1_fixed, 1)

            adds = 0
            for step in SCHEDULE:
                if step[0] == "norm":
                    hu = 2 * step[1] + step[2]
                    if hu + 2 < 2 * UNITS and hu + 2 != UNITS and hu + 2 != UNITS + 1:
                        values_of(hu + 2)
                elif step == ("v", 1, 3):
                    values_of(UNITS)
                    values_of(UNITS + 1)
                elif step[0] == "ln2":
                    n_ln2 += 1
                    rstd_of(2 + n_ln2, slice(0, TT // 2))
                elif step[0] == "w2":
                    gp.wait_ge(late_in, 80)
                    then(gp.tensor_tensor(wg_raw[:, 0:C - 1], wg_raw[:, 0:C - 1], wg_raw[:, C - 1:C].broadcast_to([E, C - 1]), ALU.subtract))
                    then(gp.memset(wg_raw[:, C - 1:C], 0.0))
                    fix_w1(0)
                    fix_w1(1)
                elif step[0] == "w1" and step[1] >= 2:
                    fix_w1(step[1])
                elif step[0] == "hidden" and step[2] > 0:
                    _, t, e = step
                    gp.wait_ge(hid_done, t * E + e + 1)
                    if e > 1:
                        gp.wait_ge(acc_done, adds)
                    adds += 1
                    gp.tensor_tensor(gacc[t % 2][:, :], gacc[t % 2][:, :], gtmp[(adds - 1) % TMP_RING][:, :], ALU.add).then_inc(acc_done, 1)

        @block.scalar
        def _(act):
            act.dma_start(wattn[:, :], wattn_d).then_inc(wattn_in, 16)
            act.dma_start(bias_row[:, :], battn_d.rearrange("(a n) -> a n", a=1)).then_inc(wattn_in, 16)
            act.dma_start(b1_rows, b1_d.rearrange("e (t p) -> (e t) p", p=P)).then_inc(wattn_in, 16)
            act.dma_start(bv_raw[:, :], battn_d[2 * C:3 * C].partition_broadcast(2)).then_inc(wattn_in, 16)
            sc = lo = hn = 0
            for step in SCHEDULE:
                kind = step[0]
                if kind == "xT":
                    _, b, n = step
                    wait_gen_full(act, step)
                    if b:
                        wait_gen_full(act, ("pv", 0, 3))
                    act.activation(xT_hi[:, PAD + 512 * n:PAD + 512 * (n + 1)], gen_bank(step)[:, :], ACT.Copy).then_inc(gen_hi, 1)
                elif kind == "qk":
                    _, b, t, n = step
                    wait_gen_full(act, step)
                    if b:
                        wait_unit_loads(act, NG - 1, QST, KST)
                        wait_unit_loads(act, NG - 2, QST, KST)
                    act.activation(arena[:, 2 * t, 512 * n:512 * (n + 1)], gen_bank(step)[:, :], ACT.Identity,
                                   bias=bias_col[:, t:t + 1]).then_inc(gen_hi, 1)
                elif kind == "v":
                    _, b, n = step
                    wait_gen_full(act, step)
                    if b:
                        act.wait_ge(vaug_ready, UNITS)
                    act.activation(vwin[:, 4 * n:4 * n + 4, :], gen_bank(step)[:, :].rearrange("p (w c) -> p w c", w=4), ACT.Copy)\
                       .then_inc(gen_act, 1)
                elif kind == "w1":
                    n = step[1]
                    wait_gen_full(act, step)
                    act.activation(w1T_hi[:, n, :], gen_bank(step)[:, :], ACT.Copy).then_inc(gen_hi, 1)
                elif kind == "x2T":
                    _, b, n = step
                    wait_gen_full(act, step)
                    act.activation(x2T[b][0][:, PAD + 512 * n:PAD + 512 * (n + 1)], gen_bank(step)[:, :], ACT.Copy).then_inc(gen_hi, 1)
                elif kind == "score":
                    _, u, i = step
                    act.wait_ge(score_full, sc + 1)
                    if i < 2:
                        if u >= 2:
                            act.wait_ge(out_done, 8 * (u - 1))
                        act.activation(probp[u % 2][:, 8 * i:8 * (i + 1), :],
                                       bank[sc % SCORE_BANKS][:, :].rearrange("p (c q) -> p c q", q=WIN), ACT.Exp).then_inc(exp_done, 1)
                    else:
                        if lo >= P_RING:
                            act.wait_ge(out_done, lo - P_RING + 1)
                        act.activation(prob[lo % P_RING][:, :, :, :],
                                       bank[sc % SCORE_BANKS][:, :].rearrange("p (c j q) -> p c j q", c=2, j=GH), ACT.Exp).then_inc(exp_done, 1)
                        lo += 1
                    sc += 1
                elif kind == "gate":
                    act.wait_ge(gsub_ready, step[1] + 1)
                    act.activation(gexp[:, :, :], gexp[:, :, :], ACT.Exp).then_inc(gexp_ready, 1)
                elif kind == "hidden":
                    act.wait_ge(hid_full, hn + 1)
                    if hn == 0:
                        act.wait_ge(out_done, 8 * UNITS)
                    if hn >= SIG_RING:
                        act.wait_ge(hid_done, hn - SIG_RING + 1)
                    act.activation(sig[hn % SIG_RING][:, :], bank[hn % HID_BANKS][:, HID:2 * HID], ACT.Sigmoid).then_inc(sig_done, 1)
                    hn += 1
                elif kind == "hidT":
                    t = step[1]
                    wait_gen_full(act, step)
                    if t >= 2:
                        wait_gen_full(act, ("y", t - 2))
                    act.activation(hidT[t % 2][:, :, :], gen_bank(step)[:, 0:HID].rearrange("p (a q) -> p a q", a=2), ACT.Copy)\
                       .then_inc(gen_act, 1)

        @block.vector
        def _(dve):
            steps = [0]

            def then(ins):
                steps[0] += 1
                ins.then_inc(dve_step, 1)
                dve.wait_ge(dve_step, steps[0])

            def layer_norm(tiles, sem_out, last_one):
                k = len(tiles)
                if lns[0]:
                    dve.wait_ge(xn_ready, min(lns[0], B))
                if lns[0] > B:
                    dve.wait_ge(ln2_ready, lns[0] - B)
                for i, t in enumerate(tiles):
                    ins = dve.bn_stats(stats[:, i, :], xres[:, t, :])
                then(ins)
                for i in range(k):
                    ins = dve.bn_aggr(mv[:, i, :], stats[:, i, :])
                then(ins)
                dve.tensor_scalar(veps[:, 0:k], mv[:, 0:k, 1], LN_EPS, None, ALU.add).then_inc(veps_ready, 1)
                lns[0] += 1
                dve.wait_ge(rstd_ready, lns[0])
                for i, t in enumerate(tiles):
                    ins = dve.tensor_scalar(xnorm[:, t, :], xres[:, t, :], mv[:, i, 0:1], rstd[:, i:i + 1], ALU.subtract, ALU.mult)
                if last_one:
                    then(ins)
                    ins = dve.memset(xnorm[:, tiles[0]:tiles[-1] + 1, C - 1:C], 1.0)
                ins.then_inc(sem_out, 1)

            lns = [0]
            dve.memset(xT_hi[:, 0:PAD].bitcast(F32), 0.0)
            dve.memset(xT_lo[:, 0:PAD].bitcast(F32), 0.0)
            then(dve.memset(xpool[:, :, :, :], 0.0))
            dve.wait_ge(wattn_in, 64)

            def by_d(ap):
                return ap.rearrange("p (g j d) -> p g d j", g=NG, j=GH)

            def by_row(ap):
                return ap.rearrange("p (g d j) -> p g d j", g=NG, j=GH)

            dve.tensor_scalar(by_row(bias_perm[:, 0:C]), by_d(bias_row[:, 0:C]), QSCALE, None, ALU.mult)
            dve.tensor_copy(by_row(bias_perm[:, C:2 * C]), by_d(bias_row[:, C:2 * C]))
            dve.tensor_scalar(by_row(wqkv[:, 0:C]), by_d(wattn[:, 0:C]), QSCALE, None, ALU.mult)
            dve.tensor_copy(by_row(wqkv[:, C:2 * C]), by_d(wattn[:, C:2 * C]))
            then(dve.tensor_copy(wqkv[:, 2 * C:3 * C], wattn[:, 2 * C:3 * C]))
            then(dve.tensor_copy(wqkv_hi[:, :], wqkv[:, :]))
            dve.tensor_tensor(wqkv_lo[:, :], wqkv[:, :], wqkv_hi[:, :].bitcast(F32), ALU.subtract)
            dve.wait_ge(const_in, 16)
            dve.tensor_copy(ident_bf[:, :], ident)
            dve.tensor_copy(band_bf[:, :], const[:, C_BAND:C_BAND + WIN])
            dve.tensor_copy(rows2[:, :], const[0:2, C_NONPAD:C_NONPAD + NB * LK + 2 * P])
            dve.tensor_copy(vpool[:, :, :, 32:64].rearrange("p c g d -> p (c g) d"),
                            const[:, C_DEN:C_DEN + 32].unsqueeze(1).broadcast_to([P, NB * NG, 32]))
            dve.memset(vpool[:, :, :, 0:32].rearrange("p c g d -> p (c g) d"), 0.0)
            then(dve.tensor_copy(bv_hi[:, :], bv_raw[:, :]))
            then(dve.tensor_tensor(bv_lo[:, :], bv_raw[:, :], bv_hi[:, :].bitcast(F32), ALU.subtract))
            then(dve.tensor_scalar(bv_lo[:, :], bv_lo[:, :], const[0:2, C_SEL + 1:C_SEL + 2], None, ALU.mult))
            dve.scalar_tensor_tensor(bv2[:, :], bv_hi[:, :].bitcast(F32), const[0:2, C_SEL:C_SEL + 1], bv_lo[:, :], ALU.mult, ALU.add)\
               .then_inc(wqkv_ready, 1)

            hn = 0
            for step in SCHEDULE:
                kind = step[0]
                if kind in GENERAL and kind not in ACT_LAST:
                    bk = gen_bank(step)
                    (wait_gen_hi if kind in ACT_FIRST else wait_gen_full)(dve, step)
                if kind == "bias":
                    dve.tensor_copy(bias_col[:, :], bk[:, 0:2])
                    dve.tensor_copy(b1_col[:, :], bk[:, P:P + 4 * E]).then_inc(gen_dve, 1)
                elif kind == "ln1":
                    b = step[1]
                    dve.wait_ge(x_in[b], 32 if b == 0 else 16)
                    layer_norm(list(range(b * TT, (b + 1) * TT)), xn_ready, False)
                elif kind == "xT":
                    _, b, n = step
                    if b:
                        dve.wait_ge(pool_ready, b)
                    cols = slice(PAD + 512 * n, PAD + 512 * (n + 1))
                    dve.tensor_reduce(pool_sum[0][:, 64 * n:64 * (n + 1)], bk[:, :].rearrange("p (a k) -> p a k", k=POOLED), AX.X, ALU.add)
                    dve.tensor_tensor(xT_lo[:, cols], bk[:, :], xT_hi[:, cols].bitcast(F32), ALU.subtract).then_inc(gen_dve, 1)
                elif kind == "pool":
                    wait_gen_done(dve, ("xT", step[1], 1))
                    for l in range(1, LEVELS):
                        pair = pool_sum[l - 1][:, :].rearrange("p (a two) -> p a two", two=2)
                        then(dve.tensor_tensor(pool_sum[l][:, :], pair[:, :, 0], pair[:, :, 1], ALU.add))
                    for l in range(LEVELS):
                        rep = 1 << l
                        n = NB // rep - 1
                        for r in range(rep):
                            ins = dve.tensor_scalar(xpool[:, rep + r:NB:rep, l, :],
                                                    pool_sum[l][:, 0:n * POOLED].rearrange("p (a k) -> p a k", k=POOLED),
                                                    1.0 / (POOLED * rep), None, ALU.mult)
                    then(ins)
                    then(dve.tensor_copy(xpool_hi[:, :, :], xpool[:, :, :, :].rearrange("p c l k -> p c (l k)")))
                    dve.tensor_tensor(xpool_lo[:, :, :], xpool[:, :, :, :].rearrange("p c l k -> p c (l k)"),
                                      xpool_hi[:, :, :].bitcast(F32), ALU.subtract).then_inc(pool_ready, 1)
                elif kind == "qk":
                    _, b, t, n = step
                    cols = slice(512 * n, 512 * (n + 1))
                    dve.scalar_tensor_tensor(arena[:, 2 * t + 1, cols], bk[:, :], bias_col[:, t:t + 1],
                                             arena[:, 2 * t, cols].bitcast(F32), ALU.add, ALU.subtract).then_inc(gen_dve, 1)
                elif kind == "kp":
                    b = step[1]
                    if b:
                        dve.wait_ge(pks_in, 48 * NG)
                    then(dve.scalar_tensor_tensor(kpool[:, :], bk[:, :], bias_col[:, 1:2], const[:, C_PADMASK:C_PADMASK + NB * LK],
                                                  ALU.add, ALU.mult))
                    then(dve.tensor_copy(kpool_hi[:, :], kpool[:, :]))
                    dve.tensor_tensor(kpool_lo[:, :], kpool[:, :], kpool_hi[:, :].bitcast(F32), ALU.subtract).then_inc(gen_dve, 1)
                elif kind == "pv":
                    _, b, n = step
                    if b:
                        dve.wait_ge(out_done, 8 * NG)
                    for j in range(GH):
                        rows = slice(j * LK, (j + 1) * LK)
                        ins = dve.tensor_scalar(vpool[rows, 4 * n:4 * n + 4, :, j * DH:(j + 1) * DH],
                                                bk[0:LK, :].rearrange("p (c g x) -> p c g x", c=4, g=NG)[:, :, :, j * DH:(j + 1) * DH],
                                                const[0:LK, C_POOLW:C_POOLW + 1], None, ALU.mult)
                    ins.then_inc(gen_dve, 1)
                elif kind == "guard":
                    _, u, m = step
                    if u and m == 0:
                        dve.wait_ge(shift_ready, u)
                    sc = bk[:, :].rearrange("p (i c j l k) -> p i c j l k", i=2, c=2, l=LEVELS, k=POOLED)
                    for i in range(2):
                        mx = lmax[:, 2 * m + i, :, :]
                        dve.tensor_reduce(mx[:, :, 1:LEVELS], sc[:, i, 0, :, 1:LEVELS, :], AX.X, ALU.max)
                    mx = lmax[:, 2 * m:2 * m + 2, :, 0]
                    dve.tensor_reduce(mx[0:WIN, :, :], sc[0:WIN, :, 0, :, 0, :], AX.X, ALU.max)
                    dve.tensor_reduce(mx[WIN:P, :, :], sc[WIN:P, :, 1, :, 0, :], AX.X, ALU.max).then_inc(gen_dve, 1)
                elif kind == "shift":
                    u = step[1]
                    wait_gen_done(dve, ("guard", u, 3))
                    if u:
                        wait_gen_full(dve, ("shiftT", u - 1))
                    dve.tensor_reduce(nshift[:, :, :].rearrange("p j i -> p i j"), lmax[:, :, :, :], AX.X, ALU.min, negate=True)\
                       .then_inc(shift_ready, 1)
                elif kind == "shiftT":
                    u = step[1]
                    if u:
                        wait_unit_loads(dve, u - 1, SHIFT)
                    then(dve.tensor_copy(nshift_hi[:, :], bk[0:GH * TT, 0:P]))
                    dve.tensor_tensor(nshift_lo[:, :], bk[0:GH * TT, 0:P], nshift_hi[:, :].bitcast(F32), ALU.subtract).then_inc(gen_dve, 1)
                elif kind == "norm":
                    _, u, h = step
                    hu, g = 2 * u + h, u % NG
                    ob = bank[3 + hu % 2]
                    dve.wait_ge(out_done, 4 * (hu + 1))
                    if hu:
                        dve.wait_ge(norm_done, hu)
                    then(dve.reciprocal(rden[0:32, :], ob[32:64, :]))
                    if u == NG and h == 0:
                        wait_gen_full(dve, ("proj", 0, 1))
                    dve.tensor_tensor(attT[32 * g:32 * (g + 1), 512 * h:512 * (h + 1)], ob[0:32, :], rden[0:32, :], ALU.mult).then_inc(norm_done, 1)
                elif kind == "proj":
                    _, b, n = step
                    tiles = slice(b * TT + 4 * n, b * TT + 4 * n + 4)
                    dve.wait_ge(xb_ready, b + 1)
                    dve.tensor_tensor(xres[:, tiles, :], xres[:, tiles, :], bk[:, :].rearrange("p (t c) -> p t c", t=4), ALU.add)\
                       .then_inc(gen_dve, 1)
                elif kind == "ln2":
                    _, b, n = step
                    wait_gen_done(dve, ("proj", b, n))
                    layer_norm(list(range(b * TT + 4 * n, b * TT + 4 * n + 4)), ln2_ready, True)
                elif kind == "w1":
                    dve.tensor_tensor(w1T_lo[:, step[1], :], bk[:, :], w1T_hi[:, step[1], :].bitcast(F32), ALU.subtract).then_inc(gen_dve, 1)
                elif kind == "w2":
                    dve.tensor_copy(woT[:, :, :], bk[:, 0:HID].rearrange("p (a c) -> p a c", a=2))
                    then(dve.tensor_copy(wgT[:, :], bk[:, HID:HID + E]))
                    then(dve.tensor_copy(wgT_hi[:, :], wgT[:, :]))
                    dve.tensor_tensor(wgT_lo[:, :], wgT[:, :], wgT_hi[:, :].bitcast(F32), ALU.subtract).then_inc(gen_dve, 1)
                elif kind == "x2T":
                    _, b, n = step
                    cols = slice(PAD + 512 * n, PAD + 512 * (n + 1))
                    dve.tensor_tensor(x2T[b][1][:, cols], bk[:, :], x2T[b][0][:, cols].bitcast(F32), ALU.subtract).then_inc(gen_dve, 1)
                elif kind == "gatelog":
                    dve.tensor_copy(glog[:, :, :], bk[:, 0:TT * E].rearrange("p (t e) -> p t e", e=E)).then_inc(gen_dve, 1)
                elif kind == "gate":
                    b = step[1]
                    wait_gen_done(dve, ("gatelog", b))
                    for t in range(TT):
                        ins = dve.max(gtop[:, t, :], glog[:, t, :])
                    then(ins)
                    for t in range(TT):
                        dve.max_index(gidx[:, t, :], gtop[:, t, :], glog[:, t, :])
                    dve.tensor_tensor(gexp[:, :, :], glog[:, :, :], gtop[:, :, 0:1].broadcast_to([P, TT, E]), ALU.subtract).then_inc(gsub_ready, 1)
                    dve.wait_ge(gexp_ready, b + 1)
                    then(dve.tensor_copy(gidx_f[:, :, :], gidx[:, :, 0:TOPK]))
                    for k in range(TOPK):
                        dve.tensor_tensor(gsel[:, k, :, :], gidx_f[:, :, k:k + 1].broadcast_to([P, TT, E]),
                                                const[:, C_IOTA:C_IOTA + E].unsqueeze(1).broadcast_to([P, TT, E]), ALU.is_equal)
                    then(dve.tensor_reduce(gsum[:, 0, :], gexp[:, :, :], AX.X, ALU.add))
                    then(dve.reciprocal(gsum[:, 1, :], gsum[:, 0, :]))
                    dve.tensor_tensor(gexp[:, :, :], gexp[:, :, :], gsum[:, 1, :].unsqueeze(2).broadcast_to([P, TT, E]), ALU.mult)
                    then(dve.tensor_tensor(gsel[:, 0, :, :], gsel[:, 0, :, :], gsel[:, 1, :, :], ALU.add))
                    then(dve.tensor_tensor(gexp[:, :, :], gexp[:, :, :], gsel[:, 0, :, :], ALU.mult))
                    then(dve.tensor_reduce(gsum[:, 2, :], gexp[:, :, :], AX.X, ALU.add))
                    then(dve.tensor_scalar(gsum[:, 2, :], gsum[:, 2, :], GATE_EPS, None, ALU.add))
                    then(dve.reciprocal(gsum[:, 3, :], gsum[:, 2, :]))
                    then(dve.tensor_tensor(comb[:, b * TT:(b + 1) * TT, :], gexp[:, :, :],
                                           gsum[:, 3, :].unsqueeze(2).broadcast_to([P, TT, E]), ALU.mult))
                    then(dve.tensor_reduce(csum[:, b * TT:(b + 1) * TT], comb[:, b * TT:(b + 1) * TT, :], AX.X, ALU.add))
                elif kind == "hidden":
                    _, t, e = step
                    dve.wait_ge(sig_done, hn + 1)
                    if e == 0:
                        if t >= 2:
                            wait_gen_full(dve, ("hidT", t - 2))
                        dst = gacc[t % 2]
                    else:
                        m = t * (E - 1) + e - 1
                        if m >= TMP_RING:
                            dve.wait_ge(acc_done, m - TMP_RING + 1)
                        dst = gtmp[m % TMP_RING]
                    dve.scalar_tensor_tensor(dst[:, :], bank[hn % HID_BANKS][:, 0:HID], comb[:, t, e:e + 1], sig[hn % SIG_RING][:, :],
                                             ALU.mult, ALU.mult).then_inc(hid_done, 1)
                    hn += 1
                elif kind == "y":
                    t = step[1]
                    if t >= 2:
                        dve.wait_ge(out_sent[t % 2], 16 * (t // 2))
                    if t:
                        wait_gen_done(dve, ("y", t - 1))
                    then(dve.scalar_tensor_tensor(ybias[:, :], bo_b[:, :], csum[:, t:t + 1], xres[:, t, :], ALU.mult, ALU.add))
                    dve.tensor_tensor(yout[t % 2][:, :], ybias[:, :], bk[:, 0:C], ALU.add).then_inc(gen_dve, 1)

        @block.tensor
        def _(pe):
            def split3(out, lhs, rhs, start=True, stop=True):
                pe.matmul(out, lhs[0], rhs[0], start=start, stop=False)
                pe.matmul(out, lhs[0], rhs[1], start=False, stop=False)
                return pe.matmul(out, lhs[1], rhs[0], start=False, stop=stop)

            wq, wk, wv = (tuple(w[:, t * C:(t + 1) * C] for w in (wqkv_hi, wqkv_lo)) for t in range(3))
            pe.wait_ge(wqkv_ready, 1)
            sc = lo = hn = 0
            for step in SCHEDULE:
                kind = step[0]
                if kind in GENERAL:
                    bk = gen_bank(step)
                    n = GEN_AT[step]
                    if n >= GEN_BANKS:
                        wait_gen_done(pe, GEN[n - GEN_BANKS])
                if kind == "bias":
                    for t in range(2):
                        ins = pe.matmul(bk[:, t:t + 1], bias_perm[0:1, t * C:(t + 1) * C], const[0:1, C_ONES:C_ONES + 1], start=True, stop=True)
                    ins = pe.transpose(bk[:, P:P + 4 * E], b1_rows, ident[0:4 * E, 0:4 * E])
                elif kind == "xT":
                    _, b, n = step
                    pe.wait_ge(xn_ready, b + 1)
                    for i in range(4):
                        ins = pe.transpose(bk[:, i * P:(i + 1) * P], xnorm[:, b * TT + 4 * n + i, :], ident)
                elif kind == "qk":
                    _, b, t, n = step
                    wait_gen_done(pe, ("xT", b, n))
                    cols = slice(PAD + 512 * n, PAD + 512 * (n + 1))
                    ins = split3(bk[:, :], (wq, wk)[t], (xT_hi[:, cols], xT_lo[:, cols]))
                elif kind == "kp":
                    pe.wait_ge(pool_ready, step[1] + 1)
                    ins = split3(bk[:, :], wk, tuple(x[:, :, :].rearrange("p c k -> p (c k)") for x in (xpool_hi, xpool_lo)))
                elif kind == "v":
                    _, b, n = step
                    wait_gen_done(pe, ("xT", b, 1))
                    for i in range(4):
                        c = 4 * n + i
                        rows = slice(c * WIN, c * WIN + P)
                        out = bk[:, i * C:(i + 1) * C]
                        split3(out, (xT_hi[:, rows], xT_lo[:, rows]), wv, stop=False)
                        one = NB * LK + (0 if c else P)
                        ins = pe.matmul(out, rows2[:, one:one + P], bv2[:, :], start=False, stop=True)
                elif kind == "pv":
                    _, b, n = step
                    pe.wait_ge(pool_ready, b + 1)
                    for i in range(4):
                        c = 4 * n + i
                        out = bk[0:LK, i * C:(i + 1) * C]
                        split3(out, (xpool_hi[:, c, :], xpool_lo[:, c, :]), wv, stop=False)
                        ins = pe.matmul(out, rows2[:, c * LK:(c + 1) * LK], bv2[:, :], start=False, stop=True)
                elif kind == "guard":
                    _, u, m = step
                    wait_unit_loads(pe, u, QST, PKM)
                    for i in range(2):
                        t = 2 * m + i
                        ins = pe.matmul(bk[:, i * 256:(i + 1) * 256], qst[u % 2][0:SR, t * P:(t + 1) * P],
                                        pkm[u % 2][0:SR, 2 * t:2 * t + 2, :, :].rearrange("p c j k -> p (c j k)"), start=True, stop=True)
                elif kind == "shiftT":
                    pe.wait_ge(shift_ready, step[1] + 1)
                    ins = pe.transpose(bk[0:GH * TT, 0:P], nshift[:, :, :].rearrange("p j i -> p (j i)"), ident)
                elif kind == "proj":
                    _, b, n = step
                    pe.wait_ge(norm_done, 2 * NG * (b + 1))
                    pe.wait_ge(late_in, 80)
                    for i in range(4):
                        t = 4 * n + i
                        ins = pe.matmul(bk[:, i * C:(i + 1) * C], attT[:, t * P:(t + 1) * P], wproj[:, :], start=True, stop=True)
                elif kind == "w1":
                    pe.wait_ge(w1_fixed, step[1] + 1)
                    if step[1] == 0:
                        wait_unit_loads(pe, UNITS - 1, QST, KST)
                        wait_unit_loads(pe, UNITS - 2, QST, KST)
                    for i in range(4):
                        ins = pe.transpose(bk[:, i * P:(i + 1) * P], w1_stage[step[1] % 2][:, i, :], ident)
                elif kind == "w2":
                    pe.wait_ge(w1_fixed, 2)
                    for i in range(2):
                        pe.transpose(bk[:, i * P:(i + 1) * P], wo_raw[:, i * P:(i + 1) * P], ident)
                    ins = pe.transpose(bk[:, HID:HID + E], wg_raw[:, :], ident[0:E, 0:E])
                elif kind == "x2T":
                    _, b, n = step
                    pe.wait_ge(ln2_ready, 2 * b + n + 1)
                    for i in range(4):
                        ins = pe.transpose(bk[:, i * P:(i + 1) * P], xnorm[:, b * TT + 4 * n + i, :], ident)
                elif kind == "gatelog":
                    b = step[1]
                    wait_gen_done(pe, ("x2T", b, 1))
                    wait_gen_done(pe, ("w2",))
                    for t in range(TT):
                        rows = slice(PAD + t * P, PAD + (t + 1) * P)
                        ins = split3(bk[:, t * E:(t + 1) * E], tuple(x[:, rows] for x in x2T[b]), (wgT_hi[:, :], wgT_lo[:, :]))
                elif kind == "hidT":
                    t = step[1]
                    pe.wait_ge(acc_done, (E - 1) * (t + 1))
                    for i in range(2):
                        ins = pe.transpose(bk[:, i * P:(i + 1) * P], gacc[t % 2][:, i * P:(i + 1) * P], ident)
                elif kind == "y":
                    t = step[1]
                    wait_gen_done(pe, ("hidT", t))
                    for i in range(2):
                        ins = pe.matmul(bk[:, 0:C], hidT[t % 2][:, i, :], woT[:, i, :], start=(i == 0), stop=(i == 1))
                elif kind == "score":
                    _, u, i = step
                    s = u % 2
                    out = bank[sc % SCORE_BANKS]
                    if sc >= SCORE_BANKS:
                        pe.wait_ge(exp_done, sc - SCORE_BANKS + 1)
                    if i == 0:
                        wait_unit_loads(pe, u, SHIFT)
                    if i < 2:
                        for k in range(8):
                            c = 8 * i + k
                            ins = pe.matmul(out[:, k * WIN:(k + 1) * WIN], pkm[s][0:SR + 2 * GH, c, :, :].rearrange("p j k -> p (j k)"),
                                            qst[s][0:SR + 2 * GH, c * WIN:(c + 1) * WIN], start=True, stop=True)
                    else:
                        if i == 2:
                            wait_unit_loads(pe, u, KST, QMK)
                        pe.matmul(out[:, :], ident_bf[:, :], band_bf[:, :].unsqueeze(1).broadcast_to([P, 2 * GH, WIN]), start=True, stop=False)
                        for k in range(2):
                            c = 2 * (i - 2) + k
                            ins = pe.matmul(out[:, k * 256:(k + 1) * 256], kst[s][0:SR + 2, c * WIN:c * WIN + P],
                                            qmk[s][0:SR + 2, :, c * WIN:(c + 1) * WIN], start=False, stop=(k == 1))
                    ins.then_inc(score_full, 1)
                    sc += 1
                elif kind == "out":
                    _, u, k = step
                    hu = 2 * u + k // 4
                    ob = bank[3 + hu % 2]
                    pe.wait_ge(exp_done, u * SPU + 2 + k + 1)
                    if k % 4 == 0:
                        pe.wait_ge(vaug_ready, hu + 1)
                        if hu >= 2:
                            pe.wait_ge(norm_done, hu - 1)
                    if k == 0 and u % NG == 0:
                        wait_gen_done(pe, ("pv", u // NG, 3))
                    for i in range(2):
                        c = 2 * k + i
                        o = ob[0:64, (c % 8) * WIN:(c % 8 + 1) * WIN]
                        for j in range(GH):
                            pe.matmul(o, vaug[hu % 2][:, c % 8, j, :], prob[lo % P_RING][:, i, j, :], start=(j == 0), stop=False)
                        ins = pe.matmul(o, vpool[:, c, u % NG, :], probp[u % 2][:, c, :], start=False, stop=True)
                    ins.then_inc(out_done, 1)
                    lo += 1
                elif kind == "hidden":
                    _, t, e = step
                    b = t // TT
                    if hn >= HID_BANKS:
                        pe.wait_ge(hid_done, hn - HID_BANKS + 1)
                    elif hn < SCORE_BANKS:
                        pe.wait_ge(exp_done, UNITS * SPU)
                    if hn == 0:
                        wait_gen_done(pe, ("w1", E - 1))
                        pe.wait_ge(norm_done, 2 * UNITS)
                    if e == 0 and t % TT == 0:
                        wait_gen_done(pe, ("x2T", b, 1))
                    rows = slice(PAD + (t % TT) * P, PAD + (t % TT + 1) * P)
                    ins = split3(bank[hn % HID_BANKS][:, :], tuple(x[:, rows] for x in x2T[b]), (w1T_hi[:, e, :], w1T_lo[:, e, :]))
                    ins.then_inc(hid_full, 1)
                    hn += 1
                if kind in GENERAL:
                    ins.then_inc(gen_full, 1)


_INS = ["L0_attn_x", "L0_attn_W_attn", "L0_attn_b_attn", "L0_attn_W_proj", "L0_attn_b_proj", "L0_ffn_Wg", "L0_ffn_W1",
        "L0_ffn_b1", "L0_ffn_Wo", "L0_ffn_bo"]


def kernel(**inputs):
    import numpy as np
    import concourse.bacc as bacc
    from concourse.bass_utils import run_bass_kernel_spmd

    nc = bacc.Bacc("TRN2", target_bir_lowering=False, num_devices=1)
    arrays, args = {}, []
    for name in _INS:
        a = np.ascontiguousarray(inputs[name])
        arrays[name] = a
        args.append(nc.dram_tensor(name, a.shape, mybir.dt.from_np(a.dtype), kind="ExternalInput").ap())
    arrays["shape_constants"] = shape_constants(np)
    args.append(nc.dram_tensor("shape_constants", (P, C_COLS), F32, kind="ExternalInput").ap())
    args.append(nc.dram_tensor("out", (B, T, C), F32, kind="ExternalOutput").ap())
    build(nc, *args)
    r = run_bass_kernel_spmd(nc, [arrays], core_ids=[0])
    return r.results[0]["out"]
```

```python
import concourse.bass as bass
from concourse import mybir
from contextlib import ExitStack

F32 = mybir.dt.float32
F32R = mybir.dt.float32r
U32 = mybir.dt.uint32
ALU = mybir.AluOpType
ACT = mybir.ActivationFunctionType
AX = mybir.AxisListType

P = 128
B, T, C = 2, 1024, 128
H, DH = 16, 8
WIN, POOLED, LEVELS = 64, 8, 4
NB = T // WIN
GH = 4
NG = H // GH
UNITS = B * NG
LK = LEVELS * POOLED
TT = T // P
SLOTS = 3
HR = GH * DH
SR = SLOTS * HR
E, HID = 8, 256
TOPK = 2
LN_EPS, GATE_EPS = 1e-5, 1e-9
QSCALE = 1.0 / float(DH) ** 0.5
PAD = WIN

C_IDENT = 0
C_BAND = C_IDENT + P
C_PADMASK = C_BAND + WIN
C_POOLW = C_PADMASK + NB * LK
C_DEN = C_POOLW + 1
C_IOTA = C_DEN + GH * DH
C_ONES = C_IOTA + E
C_SPREAD = C_ONES + P
C_ALLONE = C_SPREAD + P
C_SEL = C_ALLONE + 1
C_HEAD = C_SEL + 2
C_COLS = C_HEAD + GH


def shape_constants(np):
    c = np.zeros((P, C_COLS), np.float32)
    c[:, C_IDENT:C_IDENT + P] = np.eye(P)
    key, qry = np.arange(P)[:, None], np.arange(WIN)[None, :]
    c[:, C_BAND:C_BAND + WIN] = np.where((key > qry) & (key <= qry + WIN), np.finfo(np.float32).max, 0.0)
    blk, lev = np.arange(NB)[:, None, None], np.arange(LEVELS)[None, :, None]
    real = np.broadcast_to(blk >= 2 ** lev, (NB, LEVELS, POOLED)).reshape(-1)
    c[:, C_PADMASK:C_PADMASK + NB * LK] = real
    weight = POOLED * 2.0 ** ((np.arange(P) % LK) // POOLED)
    c[:, C_POOLW] = weight
    for j in range(GH):
        c[j * LK:(j + 1) * LK, C_DEN + j * DH:C_DEN + (j + 1) * DH] = weight[:LK, None]
    c[:, C_IOTA:C_IOTA + E] = np.arange(E)
    c[0:2, C_ONES:C_ONES + P] = 1.0
    c[0:H, C_SPREAD:C_SPREAD + C] = np.arange(C)[None, :] // DH == np.arange(H)[:, None]
    c[:, C_ALLONE] = 1.0
    c[0, C_SEL], c[1, C_SEL + 1] = 1.0, 1.0
    for r in range(SR + 2 * GH):
        c[r, C_HEAD + r % GH] = 1.0
    return c


GENERAL = {"bias", "xT", "qk", "kp", "v", "pv", "guard", "shiftT", "spread", "proj", "w1", "w2", "x2T", "gatelog", "hidT", "y"}
ACT_LAST = {"v", "hidT"}
ACT_FIRST = {"xT", "qk", "w1", "x2T"}
LAG = 3
GUARD_AT = [2, 0, 0, 5, 3, 1, 0]
HEADS_AT = {(u, (5 if u == NG - 1 else 6) + j): [(u + 2, j)] for u in range(UNITS - 2) if u + 2 != NG for j in range(GH)}
HEADS_AT.update({(NG - 1, 0): [(NG, 0), (NG, 1)], (NG - 1, 1): [(NG, 2), (NG, 3)]})
HEADS_BY_DVE = [("heads", 0, 2), ("heads", 0, 3)]
SPU = 2 + NB // 2


def schedule():
    s = [("stat", 0, 0), ("stat", 0, 1), ("apply", 0, 0), ("apply", 0, 1), ("weights",), ("xT", 0, 0), ("xT", 0, 1), ("bias",), ("pool", 0)]
    s += [("qk", 0, 0, 0), ("qk", 0, 0, 1), ("kp", 0), ("constants",), ("qk", 0, 1, 0), ("qk", 0, 1, 1)]
    s += [*[("heads", 0, j) for j in range(GH)], ("weight columns",), ("v", 0, 0), *[("guard", 0, m) for m in range(4)], ("shift", 0), ("shiftT", 0)]
    s += [("v", 0, 1), *[("heads", 1, j) for j in range(GH)]]
    unmasked, local, norms = [], [], []

    def mask():
        s.append(("mask",) + unmasked.pop(0))

    def attend():
        u, k = local.pop(0)
        s.append(("out", u, k))
        if k % 4 == 1 and norms:
            s.append(norms.pop(0))
        if k % 4 == 3:
            norms.append(("norm", u, k // 4))

    beside = {
        0: {0: [("pv", 0)], 3: [("stat", 1, 0)], 8: [("stat", 1, 1), ("apply", 1, 0)]},
        1: {2: [("apply", 1, 1)], 4: [("xT", 1, 0)], 5: [("xT", 1, 1)]},
        2: {4: [("pool", 1)], 5: [("qk", 1, 0, 0)], 6: [("qk", 1, 0, 1)], 7: [("kp", 1), ("qk", 1, 1, 0), ("qk", 1, 1, 1)]},
        3: {9: [("v", 1, 0)]},
        4: {0: [("v", 1, 1)], 2: [("norm", 3, 1)], 5: [("rden", 0)], 8: [("spread", 0, 0)],
            9: [("spread", 0, 1), ("proj", 0, 0), ("proj", 0, 1)]},
        5: {5: [("stat2", 0, 0)], 8: [("apply2", 0, 0)]},
        6: {0: [("x2T", 0, 0)], 4: [("stat2", 0, 1)], 7: [("apply2", 0, 1)], 8: [("w2",), ("x2T", 0, 1)]},
        7: {0: [("gatelog", 0, 0)], 3: [("gatelog", 0, 1)], 4: [("gatelog", 0, 2)], 5: [("gatelog", 0, 3)],
            6: [("gate", 0, 0), ("gate", 0, 1)], 8: [("gate", 0, 2)]},
    }
    for i, at in enumerate([1, 1, 2, 3, 4, 6, 7, 9]):
        beside[UNITS - 1].setdefault(at, []).append(("w1", i))
    for u in range(UNITS):
        for i in range(SPU):
            s.append(("score", u, i))
            if unmasked:
                mask()
            if i >= 2:
                local.append((u, i - 2))
                unmasked.append((u, i - 2))
            if len(local) > LAG:
                attend()
            s += beside.get(u, {}).get(i, [])
            s += [("heads",) + h for h in HEADS_AT.get((u, i), [])]
            if u + 1 < UNITS:
                first = GUARD_AT[u]
                if first <= i < first + 4:
                    s.append(("guard", u + 1, i - first))
                if i == first + 3:
                    s.append(("shift", u + 1))
                if i == first + 4:
                    s.append(("shiftT", u + 1))
        if u % NG == NG - 1:
            mask()
            while local:
                if len(local) == 1 and u == NG - 1:
                    s.append(("pv", 1))
                attend()
            if u == UNITS - 1:
                s += norms + [("gate", 0, 3)]
            norms.clear()
    beside = {
        (0, 4): [("rden", 1)], (1, 4): [("spread", 1, 0), ("spread", 1, 1)], (3, 1): [("proj", 1, 0)],
        (3, 3): [("stat2", 1, 0)], (3, 5): [("proj", 1, 1)], (4, 2): [("stat2", 1, 1)], (4, 6): [("apply2", 1, 0)],
        (4, 7): [("apply2", 1, 1)], (5, 2): [("x2T", 1, 0)], (5, 4): [("x2T", 1, 1)], (6, 0): [("gatelog", 1, 0)],
        (6, 1): [("gatelog", 1, 1)], (6, 2): [("gatelog", 1, 2), ("gatelog", 1, 3), ("gate", 1, 0), ("gate", 1, 1)],
        (6, 5): [("gate", 1, 2)], (7, 7): [("gate", 1, 3)],
    }
    for t in range(B * TT):
        for e in range(E):
            s.append(("hidden", t, e))
            s += beside.get((t, e), [])
            if t and e == 5:
                s.append(("hidT", t - 1))
            if t and e == 7:
                s.append(("y", t - 1))
    return s + [("hidT", B * TT - 1), ("y", B * TT - 1)]


SCHEDULE = schedule()
GEN = [s for s in SCHEDULE if s[0] in GENERAL]
GEN_AT = {s: n for n, s in enumerate(GEN)}
GEN_BANKS = 3
SCORE_BANKS = 3
HID_BANKS = 5
P_RING = 5
SIG_RING, TMP_RING = 3, 5
LAST_BY_PE = 2
LAST_EXPERTS = [(B * TT - 1, e) for e in range(E - LAST_BY_PE, E)]
STAGES = 4
LN_TILES = TT // 2


def build(nc, x_d, wattn_d, battn_d, wproj_d, bproj_d, wg_d, w1_d, b1_d, wo_d, bo_d, const_d, out_d):
    ctx = ExitStack()
    with ctx:
        def sb(name, shape, dt=F32):
            return ctx.enter_context(nc.sbuf_tensor(name, shape, dt))

        def sem(name):
            return ctx.enter_context(nc.semaphore(name))

        const = sb("const", [P, C_COLS])
        ident = const[:, C_IDENT:C_IDENT + P]
        band = const[:, C_BAND:C_BAND + WIN]
        rows2 = sb("rows2", [2, NB * LK + P], F32R)
        bv2 = sb("bv2", [2, C], F32R)
        bv_raw = sb("bv_raw", [2, C])
        bv_hi = sb("bv_hi", [2, C], F32R)
        bv_lo = sb("bv_lo", [2, C])
        xres = sb("xres", [P, B * TT, C])
        xnorm = sb("xnorm", [P, B * TT, C])
        attT = sb("attT", [P, T])
        denom = sb("denom", [P, T])
        wattn = attT[:, 0:3 * C]
        wqkv = attT[:, 3 * C:6 * C]
        wqkv_hi = sb("wqkv_hi", [P, 3 * C], F32R)
        wqkv_lo = sb("wqkv_lo", [P, 3 * C], F32R)
        dcomp = sb("dcomp", [P, P])
        rden = denom[0:H, :]
        bias_row = denom[0:1, 0:3 * C]
        b1_rows = denom[0:4 * E, 3 * C:4 * C]
        bias_perm = attT[0:1, 6 * C:8 * C]
        bias_col = sb("bias_col", [P, 2])
        wproj = sb("wproj", [P, C])
        bproj_b = sb("bproj_b", [P, C])
        bo_b = sb("bo_b", [P, C])
        xT_hi = sb("xT_hi", [P, PAD + T], F32R)
        xT_lo = sb("xT_lo", [P, PAD + T], F32R)
        pool_sum = [sb(f"pool_sum{l}", [P, T // (POOLED << l)]) for l in range(LEVELS)]
        xpool = sb("xpool", [P, NB, LEVELS, POOLED])
        xpool_hi = sb("xpool_hi", [P, NB, LK], F32R)
        xpool_lo = sb("xpool_lo", [P, NB, LK], F32R)
        arena = sb("arena", [P, 4, T], F32R)
        q_hi, q_lo, k_hi, k_lo = (arena[:, n, :] for n in range(4))
        kpool = sb("kpool", [P, NB * LK])
        kpool_hi = sb("kpool_hi", [P, NB * LK], F32R)
        kpool_lo = sb("kpool_lo", [P, NB * LK], F32R)
        vwin = sb("vwin", [P, NB, C])
        vpool = sb("vpool", [P, NB, NG, WIN])
        qst = [sb(f"qst{i}", [P, T], F32R) for i in range(2)]
        qmk = [sb(f"qmk{i}", [P, GH, T], F32R) for i in range(2)]
        kst = [sb(f"kst{i}", [P, PAD + T], F32R) for i in range(2)]
        pks = sb("pks", [SR, NB * LK], F32R)
        pkm = [sb(f"pkm{i}", [P, NB, GH, LK], F32R) for i in range(2)]
        vaug = [sb(f"vaug{i}", [P, NB // 2, GH, WIN]) for i in range(2)]
        work = sb("work", [P, P_RING * 512 + 2 * NB * WIN])
        prob = [work[:, i * 512:(i + 1) * 512].rearrange("p (c j q) -> p c j q", c=2, j=GH) for i in range(P_RING)]
        probp = [work[:, P_RING * 512 + i * T:P_RING * 512 + (i + 1) * T].rearrange("p (c q) -> p c q", q=WIN) for i in range(2)]
        lmax = sb("lmax", [P, TT, GH, LEVELS])
        nshift = sb("nshift", [P, GH, TT])
        nshift_parts = sb("nshift_parts", [P, 2, GH, TT], F32R)
        nshiftT = sb("nshiftT", [2 * GH * TT, P], F32R)
        stats = sb("stats", [P, TT, 6])
        mv = sb("mv", [P, TT, 2])
        veps = sb("veps", [P, TT])
        rstd = sb("rstd", [P, TT])
        nhalf = sb("nhalf", [P, TT])
        nmr = sb("nmr", [P, TT])
        w1_stage = [xpool[:, :, :, :].rearrange("p (t a) l k -> p t (a l k)", t=4), kpool[:, :].rearrange("p (t c) -> p t c", t=4),
                    xnorm[:, 0:4, :], xnorm[:, 4:8, :]]
        b1_col = sb("b1_col", [P, 4 * E])
        w1T_hi = qmk[0][:, :, :].rearrange("p a (b n) -> p (a b) n", b=2)
        w1T_lo = arena[:, :, :].rearrange("p a (b n) -> p (a b) n", b=2)
        wo_raw = sb("wo_raw", [P, HID])
        woT = sb("woT", [P, 2, C])
        wg_raw = sb("wg_raw", [E, C])
        wgT = sb("wgT", [P, E])
        wgT_hi = sb("wgT_hi", [P, E], F32R)
        wgT_lo = sb("wgT_lo", [P, E], F32R)
        x2T = [(xT_hi, xT_lo), (kst[0], kst[1])]
        glog = sb("glog", [P, TT, E])
        gtop = sb("gtop", [P, TT, 8])
        gidx = sb("gidx", [P, TT, 8], U32)
        gidx_f = sb("gidx_f", [P, TT, TOPK])
        gexp = sb("gexp", [P, TT, E])
        gsel = sb("gsel", [P, 2, TT, E])
        gsum = sb("gsum", [P, 4, TT])
        comb = sb("comb", [P, B * TT, E])
        csum = sb("csum", [P, B * TT])
        ring = [work[:, i * HID:(i + 1) * HID] for i in range(SIG_RING + TMP_RING + 4)]
        sig, gtmp = ring[0:SIG_RING], ring[SIG_RING:SIG_RING + TMP_RING]
        gacc = ring[SIG_RING + TMP_RING:SIG_RING + TMP_RING + 2]
        hidT = [r.rearrange("p (a q) -> p a q", a=2) for r in ring[SIG_RING + TMP_RING + 2:]]
        ybias = sb("ybias", [P, C])
        yout = [sb(f"yout{i}", [P, C]) for i in range(2)]

        bank = [ctx.enter_context(nc.psum_tensor(f"bank{i}", [P, 512], F32)) for i in range(8)]

        def gen_bank(step):
            return bank[5 + GEN_AT[step] % GEN_BANKS]

        x_in = [sem(f"x_in{b}") for b in range(3)]
        const_in, wattn_in, late_in = sem("const_in"), sem("wattn_in"), sem("late_in")
        w1_in = [sem(f"w1_in{i}") for i in range(STAGES)]
        cst_ready = sem("cst_ready")
        mask_done = sem("mask_done")
        xt_ready = sem("xt_ready")
        den_in, rden_ready, rden_in = sem("den_in"), sem("rden_ready"), sem("rden_in")
        zero_ready = sem("zero_ready")
        heads_ready = sem("heads_ready")
        wqkv_ready = sem("wqkv_ready")
        gen_full = sem("gen_full")
        gen_hi = sem("gen_hi")
        gen_dve = sem("gen_dve")
        gen_act = sem("gen_act")
        veps_ready, rstd_ready, nmr_ready = sem("veps_ready"), sem("rstd_ready"), sem("nmr_ready")
        xn_ready, ln2_ready = sem("xn_ready"), sem("ln2_ready")
        xb_ready = sem("xb_ready")
        pool_ready = sem("pool_ready")
        shift_ready = sem("shift_ready")
        qst_in = [sem(f"qst_in{i}") for i in range(2)]
        kst_in = [sem(f"kst_in{i}") for i in range(2)]
        qmk_in = [sem(f"qmk_in{i}") for i in range(2)]
        pv_act = sem("pv_act")
        pkm_ready = sem("pkm_ready")
        shift_in = [sem(f"shift_in{i}") for i in range(2)]
        pks_in = sem("pks_in")
        score_full, exp_done, out_done, norm_done, vaug_ready = (sem(n) for n in ("score_full", "exp_done", "out_done", "norm_done", "vaug_ready"))
        w1_fixed, wg_fixed = sem("w1_fixed"), sem("wg_fixed")
        gsub_ready, gexp_ready = sem("gsub_ready"), sem("gexp_ready")
        hid_full, sig_done, hid_done, acc_done = (sem(n) for n in ("hid_full", "sig_done", "hid_done", "acc_done"))
        out_sent = [sem(f"out_sent{i}") for i in range(2)]
        dve_step, pool_step = sem("dve_step"), sem("pool_step")

        def wait_gen_done(eng, step):
            kind = step[0] in ACT_LAST
            n = sum((s[0] in ACT_LAST) == kind for s in GEN[:GEN_AT[step] + 1])
            eng.wait_ge(gen_act if kind else gen_dve, n)

        def wait_gen_full(eng, step):
            eng.wait_ge(gen_full, GEN_AT[step] + 1)

        def wait_gen_hi(eng, step):
            eng.wait_ge(gen_hi, sum(s[0] in ACT_FIRST for s in GEN[:GEN_AT[step] + 1]))

        def wait_unit_loads(eng, u, *sems):
            for pair, n in sems:
                eng.wait_ge(pair[u % 2], 16 * n * (u // 2 + 1))

        def pv_part(eng, bk, ci, j):
            src = slice(ci * LK, (ci + 1) * LK)
            out = vpool[j * LK:(j + 1) * LK, ci:NB:4, :, j * DH:(j + 1) * DH]
            val = bk[src, :].rearrange("p (c g x) -> p c g x", c=4, g=NG)[:, :, :, j * DH:(j + 1) * DH]
            weight = const[src, C_POOLW:C_POOLW + 1]
            if ci >= 2:
                return eng.activation(out, val, ACT.Copy, scale=weight)
            return eng.tensor_scalar(out, val, weight, None, ALU.mult)

        def head_columns(eng, u, j):
            eng.wait_ge(pks_in, 48 * (u + 1))
            if u >= 2:
                eng.wait_ge(score_full, (u - 2) * SPU + 2)
            out = pkm[u % 2][0:SR, :, j, :]
            src = pks[:, :].bitcast(F32).rearrange("p (c k) -> p c k", k=LK)
            mine = const[0:SR, C_HEAD + j:C_HEAD + j + 1]
            if ("heads", u, j) in HEADS_BY_DVE:
                eng.tensor_scalar(out, src, mine, None, ALU.mult).then_inc(pkm_ready, 1)
            else:
                eng.activation(out, src, ACT.Copy, scale=mine).then_inc(pkm_ready, 1)

        PV_PARTS = [(ci, j) for ci in range(2) for j in range(GH)]

        QST, KST, QMK, SHIFT = (qst_in, 3), (kst_in, 3), (qmk_in, 4), (shift_in, 2)

        block = ctx.enter_context(nc.Block())

        @block.sync
        def _(sp):
            xv = x_d.rearrange("b (t p) c -> b p t c", p=P)
            sp.dma_start(xres[:, 0:TT // 2, :], xv[0, :, 0:TT // 2, :]).then_inc(x_in[0], 16)
            sp.dma_start(xres[:, TT // 2:TT, :], xv[0, :, TT // 2:TT, :]).then_inc(x_in[1], 16)
            sp.dma_start(const[:, :], const_d).then_inc(const_in, 16)
            sp.dma_start(xres[:, TT:2 * TT, :], xv[1]).then_inc(x_in[2], 16)
            sp.dma_start(wproj[:, :], wproj_d).then_inc(late_in, 16)
            sp.dma_start(bproj_b[:, :], bproj_d.partition_broadcast(P)).then_inc(late_in, 16)
            sp.dma_start(bo_b[:, :], bo_d.partition_broadcast(P)).then_inc(late_in, 16)
            sp.dma_start(wo_raw[:, :], wo_d).then_inc(late_in, 16)
            sp.dma_start(wg_raw[:, :], wg_d).then_inc(late_in, 16)

            def move(dst, src):
                return sp.dma_start(dst.bitcast(F32), src.bitcast(F32))

            def load_w1(n):
                sp.dma_start(w1_stage[n % STAGES], w1_d[n].rearrange("(t p) c -> p t c", p=P)).then_inc(w1_in[n % STAGES], 16)

            def load_queries(u):
                b, g, s = u // NG, u % NG, u % 2
                rows = slice(g * HR, (g + 1) * HR)
                wait_gen_done(sp, ("qk", b, 0, 1))
                if u >= 2:
                    sp.wait_ge(score_full, (u - 2) * SPU + 2)
                    wait_unit_loads(sp, u - 2, QMK)
                for n, src in enumerate((q_hi, q_hi, q_lo)):
                    move(qst[s][n * HR:(n + 1) * HR, :], src[rows, :]).then_inc(qst_in[s], 16)

            def load_pooled(u):
                b, g, s = u // NG, u % NG, u % 2
                rows = slice(g * HR, (g + 1) * HR)
                if u:
                    sp.wait_ge(pkm_ready, GH * u)
                wait_gen_done(sp, ("kp", b))
                for n, src in enumerate((kpool_hi, kpool_lo, kpool_hi)):
                    move(pks[n * HR:(n + 1) * HR, :], src[rows, :]).then_inc(pks_in, 16)

            def load_stacks(u):
                load_queries(u)
                load_pooled(u)

            def load_keys(u):
                g, s = u % NG, u % 2
                rows = slice(g * HR, (g + 1) * HR)
                wait_gen_done(sp, ("qk", u // NG, 1, 1))
                if u >= 2:
                    sp.wait_ge(score_full, (u - 1) * SPU)
                for n, src in enumerate((k_hi, k_lo, k_hi)):
                    move(kst[s][n * HR:(n + 1) * HR, PAD:], src[rows, :]).then_inc(kst_in[s], 16)

            def load_head_queries(u):
                s = u % 2
                wait_unit_loads(sp, u, QST)
                if u < 2:
                    sp.wait_ge(zero_ready, 2 * u + 2)
                for j in range(GH):
                    move(qmk[s][j:SR:GH, j, :], qst[s][j:SR:GH, :]).then_inc(qmk_in[s], 16)

            def load_local(u):
                load_keys(u)
                load_head_queries(u)

            def load_shift(u):
                s = u % 2
                wait_gen_done(sp, ("shiftT", u))
                move(qmk[s][SR:SR + 2, :, :], nshiftT[:, :]).then_inc(shift_in[s], 16)
                move(qst[s][SR:SR + 2 * GH, :], nshiftT[:, :]).then_inc(shift_in[s], 16)

            def load_denominators(b):
                sp.wait_ge(norm_done, 2 * NG * (b + 1))
                sp.dma_start(dcomp[:, :], denom[0:P:DH, :]).then_inc(den_in, 16)

            def load_reciprocals(b):
                sp.wait_ge(rden_ready, b + 1)
                sp.dma_start(rden, dcomp[:, :]).then_inc(rden_in, 16)

            load_queries(0)
            load_pooled(0)
            load_keys(0)
            load_head_queries(0)
            load_queries(1)
            for u in range(UNITS):
                load_shift(u)
                if u == 0:
                    load_pooled(1)
                if u == NG - 2:
                    load_local(u + 1)
                elif u == NG - 1:
                    load_stacks(u + 1)
                    load_stacks(u + 2)
                    load_local(u + 1)
                elif u + 1 < UNITS:
                    if u == NG:
                        load_denominators(0)
                    if u + 2 < UNITS:
                        load_stacks(u + 2)
                    if u == NG:
                        load_reciprocals(0)
                    load_local(u + 1)
                if u + 2 == UNITS:
                    wait_gen_full(sp, ("pv", 1))
                    wait_gen_full(sp, ("x2T", 0, 0))
                    for i in range(STAGES - 1):
                        load_w1(i)
            wait_gen_full(sp, ("x2T", 0, 1))
            load_w1(STAGES - 1)
            for n in range(STAGES, E):
                wait_gen_done(sp, ("w1", n - STAGES))
                load_w1(n)
            load_denominators(1)
            load_reciprocals(1)
            for t in range(B * TT):
                wait_gen_done(sp, ("y", t))
                sp.dma_start(out_d[t // TT, (t % TT) * P:(t % TT + 1) * P, :], yout[t % 2][:, :]).then_inc(out_sent[t % 2], 16)
            for i in range(2):
                sp.wait_ge(out_sent[i], 16 * B * TT // 2)

        @block.gpsimd
        def _(gp):
            steps = [0]

            def then(ins):
                steps[0] += 1
                ins.then_inc(pool_step, 1)
                gp.wait_ge(pool_step, steps[0])

            then(gp.memset(nhalf[:, :], -0.5))

            def rstd_of(n):
                cols = slice(LN_TILES * (n % 2), LN_TILES * (n % 2 + 1))
                gp.wait_ge(veps_ready, n + 1)
                gp.tensor_tensor(rstd[:, cols], veps[:, cols], nhalf[:, cols], ALU.pow).then_inc(rstd_ready, 1)
                if n >= 2 * B:
                    gp.wait_ge(rstd_ready, n + 1)
                    then(gp.tensor_tensor(nmr[:, cols], mv[:, cols, 0], rstd[:, cols], ALU.mult))
                    gp.tensor_scalar(nmr[:, cols], nmr[:, cols], -1.0, None, ALU.mult).then_inc(nmr_ready, 1)

            def add_bproj(b):
                gp.wait_ge(xn_ready, 2 * (b + 1))
                gp.wait_ge(late_in, 80)
                gp.tensor_tensor(xres[:, b * TT:(b + 1) * TT, :], xres[:, b * TT:(b + 1) * TT, :],
                                 bproj_b[:, :].unsqueeze(1).broadcast_to([P, TT, C]), ALU.add).then_inc(xb_ready, 1)

            def values_of(hu):
                u, h = hu // 2, hu % 2
                b, g = u // NG, u % NG
                if hu == 0 or hu == UNITS:
                    for n in range(2):
                        wait_gen_done(gp, ("v", b, n))
                if hu >= 2:
                    gp.wait_ge(out_done, 4 * (hu - 1))
                half = NB // 2
                for j in range(GH):
                    c0 = (g * GH + j) * DH
                    ins = gp.tensor_copy(vaug[hu % 2][:, :, j, j * DH:(j + 1) * DH], vwin[:, h * half:(h + 1) * half, c0:c0 + DH])
                ins.then_inc(vaug_ready, 1)

            def blank_keys(i):
                then(gp.memset(kst[i][:, 0:PAD].bitcast(F32), 0.0))
                gp.memset(kst[i][SR:SR + 2, :].bitcast(F32), 1.0).then_inc(zero_ready, 1)
                gp.wait_ge(zero_ready, 2 * i + 1)

            def blank_queries(i):
                gp.memset(qmk[i][:, :, :].bitcast(F32), 0.0).then_inc(zero_ready, 1)
                gp.wait_ge(zero_ready, 2 * i + 2)

            blank_keys(0)
            rstd_of(0)
            rstd_of(1)
            blank_queries(0)
            then(gp.memset(vwin[0:WIN, 0, :], 0.0))
            for i in range(2):
                then(gp.memset(vaug[i][:, :, :, :], 0.0))
                for j in range(GH):
                    ins = gp.memset(vaug[i][:, :, j, 32 + j * DH:32 + (j + 1) * DH], 1.0)
                then(ins)
                if i == 0:
                    blank_keys(1)
                    blank_queries(1)
            add_bproj(0)
            values_of(0)
            values_of(1)
            n_ln = 2

            def fix_w1(n):
                st = w1_stage[n % STAGES]
                wait_gen_done(gp, ("bias",))
                gp.wait_ge(w1_in[n % STAGES], 16 * (n // STAGES + 1))
                then(gp.tensor_tensor(st[:, :, 0:C - 1], st[:, :, 0:C - 1], st[:, :, C - 1:C].broadcast_to([P, 4, C - 1]), ALU.subtract))
                gp.tensor_copy(st[:, :, C - 1:C], b1_col[:, 4 * n:4 * n + 4].unsqueeze(2)).then_inc(w1_fixed, 1)

            adds = 0
            for step in SCHEDULE:
                if step[0] == "norm":
                    hu = 2 * step[1] + step[2]
                    if hu + 2 < 2 * UNITS and hu + 2 != UNITS and hu + 2 != UNITS + 1:
                        values_of(hu + 2)
                elif step[0] == "stat2" or (step[0] == "stat" and step[1] == 1):
                    rstd_of(n_ln)
                    n_ln += 1
                elif step == ("apply", 1, 1):
                    add_bproj(1)
                elif step == ("v", 1, 1):
                    values_of(UNITS)
                    values_of(UNITS + 1)
                elif step == ("x2T", 0, 0):
                    gp.wait_ge(late_in, 80)
                    then(gp.tensor_tensor(wg_raw[:, 0:C - 1], wg_raw[:, 0:C - 1], wg_raw[:, C - 1:C].broadcast_to([E, C - 1]), ALU.subtract))
                    gp.memset(wg_raw[:, C - 1:C], 0.0).then_inc(wg_fixed, 1)
                elif step == ("gatelog", 0, 1):
                    for n in range(STAGES):
                        fix_w1(n)
                elif step[0] == "w1" and step[1] >= STAGES:
                    fix_w1(step[1])
                elif step[0] == "hidden" and step[2] > 0 and step[1:] not in LAST_EXPERTS:
                    _, t, e = step
                    gp.wait_ge(hid_done, t * E + e + 1)
                    if e > 1:
                        gp.wait_ge(acc_done, adds)
                    adds += 1
                    gp.tensor_tensor(gacc[t % 2][:, :], gacc[t % 2][:, :], gtmp[(adds - 1) % TMP_RING][:, :], ALU.add).then_inc(acc_done, 1)

        @block.scalar
        def _(act):
            act.dma_start(wattn[:, :], wattn_d).then_inc(wattn_in, 16)
            act.dma_start(bias_row[:, :], battn_d.rearrange("(a n) -> a n", a=1)).then_inc(wattn_in, 16)
            act.dma_start(b1_rows, b1_d.rearrange("e (t p) -> (e t) p", p=P)).then_inc(wattn_in, 16)
            act.dma_start(bv_raw[:, :], battn_d[2 * C:3 * C].partition_broadcast(2)).then_inc(wattn_in, 16)
            act.wait_ge(const_in, 16)
            for i in range(2):
                act.activation(pkm[i][SR:SR + 2 * GH, :, :, :],
                               const[SR:SR + 2 * GH, C_HEAD:C_HEAD + GH].unsqueeze(1).unsqueeze(3).broadcast_to([2 * GH, NB, GH, LK]),
                               ACT.Copy).then_inc(heads_ready, 1)
            sc = lo = hn = 0
            for step in SCHEDULE:
                kind = step[0]
                if kind == "xT":
                    _, b, n = step
                    wait_gen_full(act, step)
                    if b:
                        wait_gen_full(act, ("pv", 0))
                    act.activation(xT_hi[:, PAD + 512 * n:PAD + 512 * (n + 1)], gen_bank(step)[:, :], ACT.Copy).then_inc(gen_hi, 1)
                elif kind == "qk":
                    _, b, t, n = step
                    wait_gen_full(act, step)
                    if b == 0:
                        wait_gen_done(act, ("bias",))
                    if b:
                        wait_unit_loads(act, NG - 1, QST, KST)
                        wait_unit_loads(act, NG - 2, QST, KST)
                    act.activation(arena[:, 2 * t, 512 * n:512 * (n + 1)], gen_bank(step)[:, :], ACT.Identity,
                                   bias=bias_col[:, t:t + 1]).then_inc(gen_hi, 1)
                elif kind == "v":
                    _, b, n = step
                    wait_gen_full(act, step)
                    if b:
                        act.wait_ge(vaug_ready, UNITS)
                    full = gen_bank(step)[:, :].rearrange("p (w c) -> p w c", w=4)
                    act.activation(vwin[:, 8 * n + 1:8 * n + 8:2, :], full, ACT.Copy)
                    act.activation(vwin[WIN:P, 8 * n:8 * n + 7:2, :], full[0:WIN], ACT.Copy)
                    k = 4 if n == 0 else 3
                    act.activation(vwin[0:WIN, 8 * n + 2:8 * n + 2 * k + 1:2, :], full[WIN:P, 0:k, :], ACT.Copy).then_inc(gen_act, 1)
                elif kind == "w1":
                    n = step[1]
                    wait_gen_full(act, step)
                    act.activation(w1T_hi[:, n, :], gen_bank(step)[:, :], ACT.Copy).then_inc(gen_hi, 1)
                elif kind == "x2T":
                    _, b, n = step
                    wait_gen_full(act, step)
                    act.activation(x2T[b][0][:, PAD + 512 * n:PAD + 512 * (n + 1)], gen_bank(step)[:, :], ACT.Copy).then_inc(gen_hi, 1)
                elif kind == "pv":
                    b = step[1]
                    wait_gen_full(act, step)
                    if b:
                        act.wait_ge(out_done, 8 * NG)
                    for ci, j in PV_PARTS:
                        ins = pv_part(act, gen_bank(step), ci + 2, j)
                    ins.then_inc(pv_act, 1)
                elif kind == "apply2":
                    _, b, n = step
                    act.wait_ge(nmr_ready, 2 * b + n + 1)
                    for i in range(LN_TILES):
                        o = LN_TILES * (n % 2) + i
                        act.activation(xnorm[:, b * TT + 4 * n + i, 0:C - 1], xres[:, b * TT + 4 * n + i, 0:C - 1], ACT.Identity,
                                       bias=nmr[:, o:o + 1], scale=rstd[:, o:o + 1])
                    act.activation(xnorm[:, b * TT + 4 * n:b * TT + 4 * n + 4, C - 1:C],
                                   const[:, C_ALLONE:C_ALLONE + 1].unsqueeze(1).broadcast_to([P, LN_TILES, 1]), ACT.Copy).then_inc(ln2_ready, 1)
                elif kind == "heads" and step not in HEADS_BY_DVE:
                    head_columns(act, *step[1:])
                elif kind == "score":
                    _, u, i = step
                    act.wait_ge(score_full, sc + 1)
                    if i < 2:
                        if u >= 2:
                            act.wait_ge(out_done, 8 * (u - 1))
                        act.activation(probp[u % 2][:, 8 * i:8 * (i + 1), :],
                                       bank[sc % SCORE_BANKS][:, :].rearrange("p (c q) -> p c q", q=WIN), ACT.Exp).then_inc(exp_done, 1)
                    else:
                        if lo >= P_RING:
                            act.wait_ge(out_done, lo - P_RING + 1)
                        act.activation(prob[lo % P_RING][:, :, :, :],
                                       bank[sc % SCORE_BANKS][:, :].rearrange("p (c j q) -> p c j q", c=2, j=GH), ACT.Exp).then_inc(exp_done, 1)
                        lo += 1
                    sc += 1
                elif kind == "norm":
                    _, u, h = step
                    hu, rows, cols = 2 * u + h, slice(32 * (u % NG), 32 * (u % NG + 1)), slice(512 * h, 512 * (h + 1))
                    act.wait_ge(out_done, 4 * (hu + 1))
                    if u == NG and h == 0:
                        wait_gen_full(act, ("proj", 0, 1))
                    act.activation(attT[rows, cols], bank[3 + hu % 2][0:32, :], ACT.Copy)
                    act.activation(denom[rows, cols], bank[3 + hu % 2][32:64, :], ACT.Copy).then_inc(norm_done, 1)
                elif kind == "gate" and step[2] == 0:
                    act.wait_ge(gsub_ready, step[1] + 1)
                    act.activation(gexp[:, :, :], gexp[:, :, :], ACT.Exp).then_inc(gexp_ready, 1)
                elif kind == "hidden":
                    act.wait_ge(hid_full, hn + 1)
                    if hn == 0:
                        act.wait_ge(out_done, 8 * UNITS)
                    if hn >= SIG_RING:
                        act.wait_ge(hid_done, hn - SIG_RING + 1)
                    act.activation(sig[hn % SIG_RING][:, :], bank[hn % HID_BANKS][:, HID:2 * HID], ACT.Sigmoid).then_inc(sig_done, 1)
                    hn += 1
                elif kind == "hidT":
                    t = step[1]
                    wait_gen_full(act, step)
                    if t >= 2:
                        wait_gen_full(act, ("y", t - 2))
                    act.activation(hidT[t % 2][:, :, :], gen_bank(step)[:, 0:HID].rearrange("p (a q) -> p a q", a=2), ACT.Copy)\
                       .then_inc(gen_act, 1)

        @block.vector
        def _(dve):
            steps = [0]

            def then(ins):
                steps[0] += 1
                ins.then_inc(dve_step, 1)
                dve.wait_ge(dve_step, steps[0])

            def statistics(tiles):
                done = lns[0] - 1
                if done > 0:
                    dve.wait_ge(xn_ready, min(done, 2 * B))
                if done > 2 * B:
                    dve.wait_ge(ln2_ready, done - 2 * B)
                o = LN_TILES * (lns[0] % 2)
                for i, t in enumerate(tiles):
                    ins = dve.bn_stats(stats[:, o + i, :], xres[:, t, :])
                then(ins)
                for i in range(LN_TILES):
                    ins = dve.bn_aggr(mv[:, o + i, :], stats[:, o + i, :])
                then(ins)
                dve.tensor_scalar(veps[:, o:o + LN_TILES], mv[:, o:o + LN_TILES, 1], LN_EPS, None, ALU.add).then_inc(veps_ready, 1)
                lns[0] += 1

            def normalise(tiles):
                o = LN_TILES * (lns[1] % 2)
                lns[1] += 1
                dve.wait_ge(rstd_ready, lns[1])
                for i, t in enumerate(tiles):
                    ins = dve.tensor_scalar(xnorm[:, t, :], xres[:, t, :], mv[:, o + i, 0:1], rstd[:, o + i:o + i + 1], ALU.subtract, ALU.mult)
                return ins

            def tiles_of(b, n):
                return range(b * TT + 4 * n, b * TT + 4 * n + 4)

            lns = [0, 0]

            def by_d(ap):
                return ap.rearrange("p (g j d) -> p g d j", g=NG, j=GH)

            def by_row(ap):
                return ap.rearrange("p (g d j) -> p g d j", g=NG, j=GH)

            def weights():
                dve.wait_ge(wattn_in, 64)
                dve.tensor_scalar(by_row(bias_perm[:, 0:C]), by_d(bias_row[:, 0:C]), QSCALE, None, ALU.mult)
                dve.tensor_copy(by_row(bias_perm[:, C:2 * C]), by_d(bias_row[:, C:2 * C]))
                dve.tensor_scalar(by_row(wqkv[:, 0:C]), by_d(wattn[:, 0:C]), QSCALE, None, ALU.mult)
                dve.tensor_copy(by_row(wqkv[:, C:2 * C]), by_d(wattn[:, C:2 * C]))
                then(dve.tensor_copy(wqkv[:, 2 * C:3 * C], wattn[:, 2 * C:3 * C]))
                then(dve.tensor_copy(wqkv_hi[:, :], wqkv[:, :]))
                dve.tensor_tensor(wqkv_lo[:, :], wqkv[:, :], wqkv_hi[:, :].bitcast(F32), ALU.subtract).then_inc(wqkv_ready, 1)

            def constants():
                dve.wait_ge(const_in, 16)
                dve.tensor_copy(rows2[:, 0:NB * LK], const[0:2, C_PADMASK:C_PADMASK + NB * LK])
                dve.tensor_copy(rows2[:, NB * LK:NB * LK + P], const[0:2, C_ONES:C_ONES + P])
                then(dve.tensor_copy(bv_hi[:, :], bv_raw[:, :]))
                then(dve.tensor_tensor(bv_lo[:, :], bv_raw[:, :], bv_hi[:, :].bitcast(F32), ALU.subtract))
                then(dve.tensor_scalar(bv_lo[:, :], bv_lo[:, :], const[0:2, C_SEL + 1:C_SEL + 2], None, ALU.mult))
                dve.scalar_tensor_tensor(bv2[:, :], bv_hi[:, :].bitcast(F32), const[0:2, C_SEL:C_SEL + 1], bv_lo[:, :], ALU.mult, ALU.add)\
                   .then_inc(cst_ready, 1)

            def weight_columns():
                then(dve.tensor_copy(vpool[:, :, :, 32:64].rearrange("p c g d -> p (c g) d"),
                                     const[:, C_DEN:C_DEN + 32].unsqueeze(1).broadcast_to([P, NB * NG, 32])))

            def gate(b, part):
                tiles = slice(b * TT, (b + 1) * TT)
                if part == 0:
                    wait_gen_done(dve, ("gatelog", b, 3))
                    for t in range(TT):
                        ins = dve.max(gtop[:, t, :], glog[:, t, :])
                    then(ins)
                    dve.tensor_tensor(gexp[:, :, :], glog[:, :, :], gtop[:, :, 0:1].broadcast_to([P, TT, E]), ALU.subtract).then_inc(gsub_ready, 1)
                if part == 1:
                    for t in range(TT):
                        ins = dve.max_index(gidx[:, t, :], gtop[:, t, :], glog[:, t, :])
                    then(ins)
                    then(dve.tensor_copy(gidx_f[:, :, :], gidx[:, :, 0:TOPK]))
                    for k in range(TOPK):
                        ins = dve.tensor_tensor(gsel[:, k, :, :], gidx_f[:, :, k:k + 1].broadcast_to([P, TT, E]),
                                                const[:, C_IOTA:C_IOTA + E].unsqueeze(1).broadcast_to([P, TT, E]), ALU.is_equal)
                    then(ins)
                if part == 2:
                    dve.wait_ge(gexp_ready, b + 1)
                    then(dve.tensor_reduce(gsum[:, 0, :], gexp[:, :, :], AX.X, ALU.add))
                    then(dve.reciprocal(gsum[:, 1, :], gsum[:, 0, :]))
                    dve.tensor_tensor(gexp[:, :, :], gexp[:, :, :], gsum[:, 1, :].unsqueeze(2).broadcast_to([P, TT, E]), ALU.mult)
                    then(dve.tensor_tensor(gsel[:, 0, :, :], gsel[:, 0, :, :], gsel[:, 1, :, :], ALU.add))
                    then(dve.tensor_tensor(gexp[:, :, :], gexp[:, :, :], gsel[:, 0, :, :], ALU.mult))
                if part == 3:
                    then(dve.tensor_reduce(gsum[:, 2, :], gexp[:, :, :], AX.X, ALU.add))
                    then(dve.tensor_scalar(gsum[:, 2, :], gsum[:, 2, :], GATE_EPS, None, ALU.add))
                    then(dve.reciprocal(gsum[:, 3, :], gsum[:, 2, :]))
                    then(dve.tensor_tensor(comb[:, tiles, :], gexp[:, :, :], gsum[:, 3, :].unsqueeze(2).broadcast_to([P, TT, E]), ALU.mult))
                    then(dve.tensor_reduce(csum[:, tiles], comb[:, tiles, :], AX.X, ALU.add))

            dve.memset(xT_hi[:, 0:PAD].bitcast(F32), 0.0)
            dve.memset(xT_lo[:, 0:PAD].bitcast(F32), 0.0)
            dve.memset(vpool[:, :, :, 0:32].rearrange("p c g d -> p (c g) d"), 0.0)
            then(dve.memset(xpool[:, :, :, :], 0.0))
            hn = lo = 0
            for step in SCHEDULE:
                kind = step[0]
                if kind in GENERAL and kind not in ACT_LAST:
                    bk = gen_bank(step)
                    (wait_gen_hi if kind in ACT_FIRST else wait_gen_full)(dve, step)
                if kind == "bias":
                    dve.tensor_copy(bias_col[:, :], bk[:, 0:2])
                    dve.tensor_copy(b1_col[:, :], bk[:, P:P + 4 * E]).then_inc(gen_dve, 1)
                elif kind == "weights":
                    weights()
                elif kind == "constants":
                    constants()
                elif kind == "weight columns":
                    weight_columns()
                elif kind == "stat":
                    _, b, n = step
                    dve.wait_ge(x_in[n if b == 0 else 2], 16)
                    statistics(tiles_of(b, n))
                elif kind == "apply":
                    normalise(tiles_of(*step[1:])).then_inc(xn_ready, 1)
                elif kind == "xT":
                    _, b, n = step
                    if b:
                        dve.wait_ge(pool_ready, b)
                    cols = slice(PAD + 512 * n, PAD + 512 * (n + 1))
                    dve.tensor_tensor(xT_lo[:, cols], bk[:, :], xT_hi[:, cols].bitcast(F32), ALU.subtract).then_inc(xt_ready, 1)
                    dve.tensor_reduce(pool_sum[0][:, 64 * n:64 * (n + 1)], bk[:, :].rearrange("p (a k) -> p a k", k=POOLED), AX.X, ALU.add)\
                       .then_inc(gen_dve, 1)
                elif kind == "pool":
                    wait_gen_done(dve, ("xT", step[1], 1))
                    for l in range(1, LEVELS):
                        pair = pool_sum[l - 1][:, :].rearrange("p (a two) -> p a two", two=2)
                        then(dve.tensor_tensor(pool_sum[l][:, :], pair[:, :, 0], pair[:, :, 1], ALU.add))
                    for l in range(LEVELS):
                        rep = 1 << l
                        n = NB // rep - 1
                        ins = dve.tensor_scalar(xpool[:, rep:NB, l, :].rearrange("p (a r) k -> p a r k", r=rep),
                                                pool_sum[l][:, 0:n * POOLED].rearrange("p (a k) -> p a k", k=POOLED)
                                                .unsqueeze(2).broadcast_to([P, n, rep, POOLED]),
                                                1.0 / (POOLED * rep), None, ALU.mult)
                    then(ins)
                    then(dve.tensor_copy(xpool_hi[:, :, :], xpool[:, :, :, :].rearrange("p c l k -> p c (l k)")))
                    dve.tensor_tensor(xpool_lo[:, :, :], xpool[:, :, :, :].rearrange("p c l k -> p c (l k)"),
                                      xpool_hi[:, :, :].bitcast(F32), ALU.subtract).then_inc(pool_ready, 1)
                elif kind == "qk":
                    _, b, t, n = step
                    cols = slice(512 * n, 512 * (n + 1))
                    dve.scalar_tensor_tensor(arena[:, 2 * t + 1, cols], bk[:, :], bias_col[:, t:t + 1],
                                             arena[:, 2 * t, cols].bitcast(F32), ALU.add, ALU.subtract).then_inc(gen_dve, 1)
                elif kind == "kp":
                    b = step[1]
                    if b:
                        dve.wait_ge(pks_in, 48 * NG)
                    then(dve.scalar_tensor_tensor(kpool[:, :], bk[:, :], bias_col[:, 1:2], const[:, C_PADMASK:C_PADMASK + NB * LK],
                                                  ALU.add, ALU.mult))
                    then(dve.tensor_copy(kpool_hi[:, :], kpool[:, :]))
                    dve.tensor_tensor(kpool_lo[:, :], kpool[:, :], kpool_hi[:, :].bitcast(F32), ALU.subtract).then_inc(gen_dve, 1)
                elif kind == "pv":
                    b = step[1]
                    if b:
                        dve.wait_ge(out_done, 8 * NG)
                    for ci, j in PV_PARTS[:-1]:
                        pv_part(dve, bk, ci, j)
                    dve.wait_ge(pv_act, b + 1)
                    pv_part(dve, bk, *PV_PARTS[-1]).then_inc(gen_dve, 1)
                elif kind == "guard":
                    _, u, m = step
                    if u and m == 0:
                        dve.wait_ge(shift_ready, u)
                    sc = bk[:, :].rearrange("p (i c j l k) -> p i c j l k", i=2, c=2, l=LEVELS, k=POOLED)
                    for i in range(2):
                        mx = lmax[:, 2 * m + i, :, :]
                        dve.tensor_reduce(mx[:, :, 1:LEVELS], sc[:, i, 0, :, 1:LEVELS, :], AX.X, ALU.max)
                    mx = lmax[:, 2 * m:2 * m + 2, :, 0]
                    dve.tensor_reduce(mx[0:WIN, :, :], sc[0:WIN, :, 0, :, 0, :], AX.X, ALU.max)
                    dve.tensor_reduce(mx[WIN:P, :, :], sc[WIN:P, :, 1, :, 0, :], AX.X, ALU.max).then_inc(gen_dve, 1)
                elif kind == "shift":
                    u = step[1]
                    wait_gen_done(dve, ("guard", u, 3))
                    if u:
                        wait_gen_full(dve, ("shiftT", u - 1))
                    then(dve.tensor_reduce(nshift[:, :, :].rearrange("p j i -> p i j"), lmax[:, :, :, :], AX.X, ALU.min, negate=True))
                    then(dve.tensor_copy(nshift_parts[:, 0, :, :], nshift[:, :, :]))
                    dve.tensor_tensor(nshift_parts[:, 1, :, :], nshift[:, :, :], nshift_parts[:, 0, :, :].bitcast(F32), ALU.subtract)\
                       .then_inc(shift_ready, 1)
                elif kind == "shiftT":
                    u = step[1]
                    if u:
                        wait_unit_loads(dve, u - 1, SHIFT)
                    dve.tensor_copy(nshiftT[:, :], bk[0:2 * GH * TT, 0:P]).then_inc(gen_dve, 1)
                elif step in HEADS_BY_DVE:
                    head_columns(dve, *step[1:])
                elif kind == "mask":
                    _, u, k = step
                    dve.wait_ge(exp_done, u * SPU + 2 + k + 1)
                    dve.tensor_tensor(prob[lo % P_RING][:, :, :, :].rearrange("p c j q -> p (c j) q"),
                                      prob[lo % P_RING][:, :, :, :].rearrange("p c j q -> p (c j) q"),
                                      band.unsqueeze(1).broadcast_to([P, 2 * GH, WIN]), ALU.min).then_inc(mask_done, 1)
                    lo += 1
                elif kind == "rden":
                    dve.wait_ge(den_in, 16 * (step[1] + 1))
                    dve.reciprocal(dcomp[:, :], dcomp[:, :]).then_inc(rden_ready, 1)
                elif kind == "spread":
                    _, b, h = step
                    cols = slice(512 * h, 512 * (h + 1))
                    dve.wait_ge(norm_done, 2 * NG * (b + 1))
                    dve.tensor_tensor(attT[:, cols], attT[:, cols], bk[:, :], ALU.mult).then_inc(gen_dve, 1)
                elif kind == "proj":
                    _, b, n = step
                    tiles = slice(b * TT + 4 * n, b * TT + 4 * n + 4)
                    dve.wait_ge(xb_ready, b + 1)
                    dve.tensor_tensor(xres[:, tiles, :], xres[:, tiles, :], bk[:, :].rearrange("p (t c) -> p t c", t=4), ALU.add)\
                       .then_inc(gen_dve, 1)
                elif kind == "stat2":
                    _, b, n = step
                    wait_gen_done(dve, ("proj", b, n))
                    statistics(tiles_of(b, n))
                elif kind == "w1":
                    dve.tensor_tensor(w1T_lo[:, step[1], :], bk[:, :], w1T_hi[:, step[1], :].bitcast(F32), ALU.subtract).then_inc(gen_dve, 1)
                elif kind == "w2":
                    dve.tensor_copy(woT[:, :, :], bk[:, 0:HID].rearrange("p (a c) -> p a c", a=2))
                    then(dve.tensor_copy(wgT[:, :], bk[:, HID:HID + E]))
                    then(dve.tensor_copy(wgT_hi[:, :], wgT[:, :]))
                    dve.tensor_tensor(wgT_lo[:, :], wgT[:, :], wgT_hi[:, :].bitcast(F32), ALU.subtract).then_inc(gen_dve, 1)
                elif kind == "x2T":
                    _, b, n = step
                    cols = slice(PAD + 512 * n, PAD + 512 * (n + 1))
                    dve.tensor_tensor(x2T[b][1][:, cols], bk[:, :], x2T[b][0][:, cols].bitcast(F32), ALU.subtract).then_inc(gen_dve, 1)
                elif kind == "gatelog":
                    n = step[2]
                    dve.tensor_copy(glog[:, 2 * n:2 * n + 2, :], bk[:, 2 * n * E:(2 * n + 2) * E].rearrange("p (t e) -> p t e", e=E)).then_inc(gen_dve, 1)
                elif kind == "gate":
                    gate(*step[1:])
                elif kind == "hidden":
                    _, t, e = step
                    dve.wait_ge(sig_done, hn + 1)
                    if e == 0:
                        if t >= 2:
                            wait_gen_full(dve, ("hidT", t - 2))
                        dst = gacc[t % 2]
                    else:
                        m = t * (E - 1) + e - 1
                        if m >= TMP_RING:
                            dve.wait_ge(acc_done, m - TMP_RING + 1)
                        dst = gtmp[m % TMP_RING]
                    dve.scalar_tensor_tensor(dst[:, :], bank[hn % HID_BANKS][:, 0:HID], comb[:, t, e:e + 1], sig[hn % SIG_RING][:, :],
                                             ALU.mult, ALU.mult).then_inc(hid_done, 1)
                    hn += 1
                elif kind == "y":
                    t = step[1]
                    if t >= 2:
                        dve.wait_ge(out_sent[t % 2], 16 * (t // 2))
                    if t:
                        wait_gen_done(dve, ("y", t - 1))
                    then(dve.scalar_tensor_tensor(ybias[:, :], bo_b[:, :], csum[:, t:t + 1], xres[:, t, :], ALU.mult, ALU.add))
                    dve.tensor_tensor(yout[t % 2][:, :], ybias[:, :], bk[:, 0:C], ALU.add).then_inc(gen_dve, 1)

        @block.tensor
        def _(pe):
            def split3(out, lhs, rhs, start=True, stop=True):
                pe.matmul(out, lhs[0], rhs[0], start=start, stop=False)
                pe.matmul(out, lhs[0], rhs[1], start=False, stop=False)
                return pe.matmul(out, lhs[1], rhs[0], start=False, stop=stop)

            wq, wk, wv = (tuple(w[:, t * C:(t + 1) * C] for w in (wqkv_hi, wqkv_lo)) for t in range(3))
            sc = lo = hn = 0
            for step in SCHEDULE:
                kind = step[0]
                if kind in GENERAL:
                    bk = gen_bank(step)
                    n = GEN_AT[step]
                    if n >= GEN_BANKS:
                        wait_gen_done(pe, GEN[n - GEN_BANKS])
                if kind == "bias":
                    pe.wait_ge(wqkv_ready, 1)
                    for t in range(2):
                        ins = pe.matmul(bk[:, t:t + 1], bias_perm[0:1, t * C:(t + 1) * C], const[0:1, C_ONES:C_ONES + 1], start=True, stop=True)
                    ins = pe.transpose(bk[:, P:P + 4 * E], b1_rows, ident[0:4 * E, 0:4 * E])
                elif kind == "xT":
                    _, b, n = step
                    pe.wait_ge(xn_ready, 2 * b + n + 1)
                    if b == n == 0:
                        pe.wait_ge(const_in, 16)
                    for i in range(4):
                        ins = pe.transpose(bk[:, i * P:(i + 1) * P], xnorm[:, b * TT + 4 * n + i, :], ident)
                elif kind == "qk":
                    _, b, t, n = step
                    pe.wait_ge(xt_ready, 2 * b + n + 1)
                    cols = slice(PAD + 512 * n, PAD + 512 * (n + 1))
                    ins = split3(bk[:, :], (wq, wk)[t], (xT_hi[:, cols], xT_lo[:, cols]))
                elif kind == "kp":
                    pe.wait_ge(pool_ready, step[1] + 1)
                    ins = split3(bk[:, :], wk, tuple(x[:, :, :].rearrange("p c k -> p (c k)") for x in (xpool_hi, xpool_lo)))
                elif kind == "v":
                    _, b, n = step
                    pe.wait_ge(cst_ready, 1)
                    pe.wait_ge(xt_ready, 2 * b + n + 1)
                    for i in range(4):
                        t = 4 * n + i
                        rows = slice(PAD + t * P, PAD + (t + 1) * P)
                        out = bk[:, i * C:(i + 1) * C]
                        split3(out, (xT_hi[:, rows], xT_lo[:, rows]), wv, stop=False)
                        ins = pe.matmul(out, rows2[:, NB * LK:NB * LK + P], bv2[:, :], start=False, stop=True)
                elif kind == "pv":
                    pe.wait_ge(cst_ready, 1)
                    for i in range(4):
                        out = bk[:, i * C:(i + 1) * C]
                        split3(out, tuple(x[:, 4 * i:4 * i + 4, :].rearrange("p c k -> p (c k)") for x in (xpool_hi, xpool_lo)), wv, stop=False)
                        ins = pe.matmul(out, rows2[:, 4 * i * LK:4 * (i + 1) * LK], bv2[:, :], start=False, stop=True)
                elif kind == "guard":
                    _, u, m = step
                    wait_unit_loads(pe, u, QST)
                    pe.wait_ge(pkm_ready, GH * (u + 1))
                    for i in range(2):
                        t = 2 * m + i
                        ins = pe.matmul(bk[:, i * 256:(i + 1) * 256], qst[u % 2][0:SR, t * P:(t + 1) * P],
                                        pkm[u % 2][0:SR, 2 * t:2 * t + 2, :, :].rearrange("p c j k -> p (c j k)"), start=True, stop=True)
                elif kind == "shiftT":
                    pe.wait_ge(shift_ready, step[1] + 1)
                    ins = pe.transpose(bk[0:2 * GH * TT, 0:P], nshift_parts[:, :, :, :].bitcast(F32).rearrange("p n j i -> p (n j i)"), ident)
                elif kind == "spread":
                    _, b, n = step
                    pe.wait_ge(rden_in, 16 * (b + 1))
                    ins = pe.matmul(bk[:, :], const[0:H, C_SPREAD:C_SPREAD + C], rden[:, 512 * n:512 * (n + 1)], start=True, stop=True)
                elif kind == "proj":
                    _, b, n = step
                    wait_gen_done(pe, ("spread", b, n))
                    pe.wait_ge(late_in, 80)
                    for i in range(4):
                        t = 4 * n + i
                        ins = pe.matmul(bk[:, i * C:(i + 1) * C], attT[:, t * P:(t + 1) * P], wproj[:, :], start=True, stop=True)
                elif kind == "w1":
                    pe.wait_ge(w1_fixed, step[1] + 1)
                    if step[1] == 0:
                        wait_unit_loads(pe, UNITS - 1, QST, KST)
                        wait_unit_loads(pe, UNITS - 2, QST, KST)
                    for i in range(4):
                        ins = pe.transpose(bk[:, i * P:(i + 1) * P], w1_stage[step[1] % STAGES][:, i, :], ident)
                elif kind == "w2":
                    pe.wait_ge(wg_fixed, 1)
                    for i in range(2):
                        pe.transpose(bk[:, i * P:(i + 1) * P], wo_raw[:, i * P:(i + 1) * P], ident)
                    ins = pe.transpose(bk[:, HID:HID + E], wg_raw[:, :], ident[0:E, 0:E])
                elif kind == "x2T":
                    _, b, n = step
                    pe.wait_ge(ln2_ready, 2 * b + n + 1)
                    for i in range(4):
                        ins = pe.transpose(bk[:, i * P:(i + 1) * P], xnorm[:, b * TT + 4 * n + i, :], ident)
                elif kind == "gatelog":
                    _, b, n = step
                    wait_gen_done(pe, ("x2T", b, 1))
                    wait_gen_done(pe, ("w2",))
                    for t in (2 * n, 2 * n + 1):
                        rows = slice(PAD + t * P, PAD + (t + 1) * P)
                        ins = split3(bk[:, t * E:(t + 1) * E], tuple(x[:, rows] for x in x2T[b]), (wgT_hi[:, :], wgT_lo[:, :]))
                elif kind == "hidT":
                    t = step[1]
                    if t < B * TT - 1:
                        pe.wait_ge(acc_done, (E - 1) * (t + 1))
                        for i in range(2):
                            ins = pe.transpose(bk[:, i * P:(i + 1) * P], gacc[t % 2][:, i * P:(i + 1) * P], ident)
                    else:
                        pe.wait_ge(hid_done, E * B * TT)
                        rest = [gtmp[(t * (E - 1) + e - 1) % TMP_RING] for _, e in LAST_EXPERTS]
                        for i in range(2):
                            for k, src in enumerate(rest):
                                ins = pe.matmul(bk[:, i * P:(i + 1) * P], src[:, i * P:(i + 1) * P], ident, start=(i == k == 0), stop=False)
                        pe.wait_ge(acc_done, (E - 1) * (t + 1) - LAST_BY_PE)
                        for i in range(2):
                            ins = pe.matmul(bk[:, i * P:(i + 1) * P], gacc[t % 2][:, i * P:(i + 1) * P], ident, start=False, stop=(i == 1))
                elif kind == "y":
                    t = step[1]
                    wait_gen_done(pe, ("hidT", t))
                    for i in range(2):
                        ins = pe.matmul(bk[:, 0:C], hidT[t % 2][:, i, :], woT[:, i, :], start=(i == 0), stop=(i == 1))
                elif kind == "score":
                    _, u, i = step
                    s = u % 2
                    out = bank[sc % SCORE_BANKS]
                    if sc >= SCORE_BANKS:
                        pe.wait_ge(exp_done, sc - SCORE_BANKS + 1)
                    if i == 0:
                        pe.wait_ge(heads_ready, min(u, 1) + 1)
                        wait_unit_loads(pe, u, SHIFT)
                    if i < 2:
                        for k in range(8):
                            c = 8 * i + k
                            ins = pe.matmul(out[:, k * WIN:(k + 1) * WIN], pkm[s][0:SR + 2 * GH, c, :, :].rearrange("p j k -> p (j k)"),
                                            qst[s][0:SR + 2 * GH, c * WIN:(c + 1) * WIN], start=True, stop=True)
                    else:
                        if i == 2:
                            wait_unit_loads(pe, u, KST, QMK)
                        for k in range(2):
                            c = 2 * (i - 2) + k
                            ins = pe.matmul(out[:, k * 256:(k + 1) * 256], kst[s][0:SR + 2, c * WIN:c * WIN + P],
                                            qmk[s][0:SR + 2, :, c * WIN:(c + 1) * WIN], start=True, stop=True)
                    ins.then_inc(score_full, 1)
                    sc += 1
                elif kind == "out":
                    _, u, k = step
                    hu = 2 * u + k // 4
                    ob = bank[3 + hu % 2]
                    pe.wait_ge(mask_done, lo + 1)
                    if k % 4 == 0:
                        pe.wait_ge(vaug_ready, hu + 1)
                        if hu >= 2:
                            pe.wait_ge(norm_done, hu - 1)
                    if k == 0 and u % NG == 0:
                        wait_gen_done(pe, ("pv", u // NG))
                    for i in range(2):
                        c = 2 * k + i
                        o = ob[0:64, (c % 8) * WIN:(c % 8 + 1) * WIN]
                        for j in range(GH):
                            pe.matmul(o, vaug[hu % 2][:, c % 8, j, :], prob[lo % P_RING][:, i, j, :], start=(j == 0), stop=False)
                        ins = pe.matmul(o, vpool[:, c, u % NG, :], probp[u % 2][:, c, :], start=False, stop=True)
                    ins.then_inc(out_done, 1)
                    lo += 1
                elif kind == "hidden":
                    _, t, e = step
                    b = t // TT
                    if hn >= HID_BANKS:
                        pe.wait_ge(hid_done, hn - HID_BANKS + 1)
                    elif hn == 0:
                        pe.wait_ge(exp_done, UNITS * SPU)
                    elif hn == SCORE_BANKS:
                        pe.wait_ge(norm_done, 2 * UNITS)
                    if hn == 0:
                        wait_gen_done(pe, ("w1", E - 1))
                    if e == 0 and t % TT == 0:
                        wait_gen_done(pe, ("x2T", b, 1))
                    rows = slice(PAD + (t % TT) * P, PAD + (t % TT + 1) * P)
                    ins = split3(bank[hn % HID_BANKS][:, :], tuple(x[:, rows] for x in x2T[b]), (w1T_hi[:, e, :], w1T_lo[:, e, :]))
                    ins.then_inc(hid_full, 1)
                    hn += 1
                if kind in GENERAL:
                    ins.then_inc(gen_full, 1)


_INS = ["L0_attn_x", "L0_attn_W_attn", "L0_attn_b_attn", "L0_attn_W_proj", "L0_attn_b_proj", "L0_ffn_Wg", "L0_ffn_W1",
        "L0_ffn_b1", "L0_ffn_Wo", "L0_ffn_bo"]


def kernel(**inputs):
    import numpy as np
    import concourse.bacc as bacc
    from concourse.bass_utils import run_bass_kernel_spmd

    nc = bacc.Bacc("TRN2", target_bir_lowering=False, num_devices=1)
    arrays, args = {}, []
    for name in _INS:
        a = np.ascontiguousarray(inputs[name])
        arrays[name] = a
        args.append(nc.dram_tensor(name, a.shape, mybir.dt.from_np(a.dtype), kind="ExternalInput").ap())
    arrays["shape_constants"] = shape_constants(np)
    args.append(nc.dram_tensor("shape_constants", (P, C_COLS), F32, kind="ExternalInput").ap())
    args.append(nc.dram_tensor("out", (B, T, C), F32, kind="ExternalOutput").ap())
    build(nc, *args)
    r = run_bass_kernel_spmd(nc, [arrays], core_ids=[0])
    return r.results[0]["out"]
```
